# Optimizing a Trainium2 kernel written in Bass

```python
import numpy as np
import jax
import jax.numpy as jnp

def _softmax(x, axis=-1):
    return jax.nn.softmax(x, axis=axis)

def _gelu(x):
    return jax.nn.gelu(x, approximate=True)

def _silu(x):
    return jax.nn.silu(x)

def _sigmoid(x):
    return jax.nn.sigmoid(x)

def _layernorm(x, axis=-1, eps=1e-05):
    m = jnp.mean(x, axis=axis, keepdims=True)
    v = jnp.var(x, axis=axis, keepdims=True)
    return (x - m) / jnp.sqrt(v + eps)

def _scatter_add(tgt, idx, src, axis=0):
    return tgt.at[idx].add(src)

def _segment_sum(src, seg, n):
    return jax.ops.segment_sum(src, seg, n)
kernel_name = 'mk_prb_d1_jaxref_r8_a7b6a9'

def setup_inputs(seed: int=0):
    np.random.seed(seed)
    _w = jnp.asarray

    def _L0_attn_setup():
        import jax, jax.numpy as jnp
        import numpy as np
        DIM = 128
        B, S = (8, 256)
        LN_EPS = 1e-05
        key = jax.random.key(seed)
        k1, k2, k3 = jax.random.split(key, 3)
        x = jax.random.normal(k1, (B, S, DIM), dtype=jnp.float32)
        w_qkv = jax.random.normal(k2, (3 * DIM, DIM), dtype=jnp.float32) * np.sqrt(2.0 / (DIM + 3 * DIM))
        w_fc = jax.random.normal(k3, (DIM, DIM), dtype=jnp.float32) * np.sqrt(2.0 / (DIM + DIM))
        b_fc = jnp.zeros((DIM,), dtype=jnp.float32)
        gamma = jnp.ones((DIM,), dtype=jnp.float32)
        beta = jnp.zeros((DIM,), dtype=jnp.float32)
        return {'x': x, 'w_qkv': w_qkv, 'w_fc': w_fc, 'b_fc': b_fc, 'gamma': gamma, 'beta': beta}
    _L0_attn_in = _L0_attn_setup()

    def _L0_ffn_setup():
        import jax, jax.numpy as jnp
        import numpy as np
        DIM = 128
        HEADS = 16
        HD = DIM // HEADS
        M = 32
        E = 4
        K = 2
        HID = 256
        MID = 256
        LB = 0.01
        EPS = 1.1920929e-07

        def _rms(x, w):
            return x * jax.lax.rsqrt(jnp.mean(x * x, axis=-1, keepdims=True) + EPS) * w

        def _gelu(x):
            return jax.nn.gelu(x, approximate=False)
        key = jax.random.key(seed)
        ks = jax.random.split(key, 20)
        d = DIM
        w = lambda k, s: jax.random.normal(k, s, jnp.float32) * 0.02
        return {'x': jax.random.normal(ks[0], (4, 128, d), jnp.float32), 'n1_w': jnp.ones((d,), jnp.float32), 'n2_w': jnp.ones((d,), jnp.float32), 'wq': w(ks[1], (d, d)), 'wk': w(ks[2], (d, d)), 'wv': w(ks[3], (d, d)), 'wo': w(ks[4], (d, d)), 'qn_w': jnp.ones((HD,), jnp.float32), 'kn_w': jnp.ones((HD,), jnp.float32), 'gate_w': w(ks[5], (E, d)), 'e0_up': w(ks[6], (HID, d)), 'e0_down': w(ks[7], (d, HID)), 'e1_w1': w(ks[8], (HID, d)), 'e1_w2': w(ks[9], (HID, d)), 'e1_down': w(ks[10], (d, HID)), 'e2_l1': w(ks[11], (MID, d)), 'e2_l2': w(ks[12], (HID, MID)), 'e2_l3': w(ks[13], (MID, HID)), 'e2_l4': w(ks[14], (d, MID)), 'e3_down': w(ks[15], (d, d)), 'e3_up': w(ks[16], (HID, d)), 'e3_out': w(ks[17], (d, HID))}
    _L0_ffn_in = _L0_ffn_setup()
    _d = {'L0_attn_x': _L0_attn_in['x'], 'L0_attn_w_qkv': _L0_attn_in['w_qkv'], 'L0_attn_w_fc': _L0_attn_in['w_fc'], 'L0_attn_b_fc': _L0_attn_in['b_fc'], 'L0_attn_gamma': _L0_attn_in['gamma'], 'L0_attn_beta': _L0_attn_in['beta'], 'L0_ffn_n1_w': _L0_ffn_in['n1_w'], 'L0_ffn_n2_w': _L0_ffn_in['n2_w'], 'L0_ffn_wq': _L0_ffn_in['wq'], 'L0_ffn_wk': _L0_ffn_in['wk'], 'L0_ffn_wv': _L0_ffn_in['wv'], 'L0_ffn_wo': _L0_ffn_in['wo'], 'L0_ffn_qn_w': _L0_ffn_in['qn_w'], 'L0_ffn_kn_w': _L0_ffn_in['kn_w'], 'L0_ffn_gate_w': _L0_ffn_in['gate_w'], 'L0_ffn_e0_up': _L0_ffn_in['e0_up'], 'L0_ffn_e0_down': _L0_ffn_in['e0_down'], 'L0_ffn_e1_w1': _L0_ffn_in['e1_w1'], 'L0_ffn_e1_w2': _L0_ffn_in['e1_w2'], 'L0_ffn_e1_down': _L0_ffn_in['e1_down'], 'L0_ffn_e2_l1': _L0_ffn_in['e2_l1'], 'L0_ffn_e2_l2': _L0_ffn_in['e2_l2'], 'L0_ffn_e2_l3': _L0_ffn_in['e2_l3'], 'L0_ffn_e2_l4': _L0_ffn_in['e2_l4'], 'L0_ffn_e3_down': _L0_ffn_in['e3_down'], 'L0_ffn_e3_up': _L0_ffn_in['e3_up'], 'L0_ffn_e3_out': _L0_ffn_in['e3_out']}
    _x0 = _d['L0_attn_x']
    _d['L0_attn_x'] = jax.random.normal(jax.random.fold_in(jax.random.key(seed), 1), (8, 256, 128), dtype=_x0.dtype)
    del _x0
    return _d

def reference(L0_attn_x, L0_attn_w_qkv, L0_attn_w_fc, L0_attn_b_fc, L0_attn_gamma, L0_attn_beta, L0_ffn_n1_w, L0_ffn_n2_w, L0_ffn_wq, L0_ffn_wk, L0_ffn_wv, L0_ffn_wo, L0_ffn_qn_w, L0_ffn_kn_w, L0_ffn_gate_w, L0_ffn_e0_up, L0_ffn_e0_down, L0_ffn_e1_w1, L0_ffn_e1_w2, L0_ffn_e1_down, L0_ffn_e2_l1, L0_ffn_e2_l2, L0_ffn_e2_l3, L0_ffn_e2_l4, L0_ffn_e3_down, L0_ffn_e3_up, L0_ffn_e3_out):

    def _L0_attn_ref(x, w_qkv, w_fc, b_fc, gamma, beta):
        import jax, jax.numpy as jnp
        import numpy as np
        DIM = 128
        B, S = (8, 256)
        LN_EPS = 1e-05
        scaling = DIM ** (-0.5)
        qkv = jnp.einsum('bsd,ed->bse', x, w_qkv)
        q, k, v = jnp.split(qkv, 3, axis=-1)
        att = jax.nn.softmax(jnp.einsum('bqd,bkd->bqk', q, k) * scaling, axis=-1)
        y = jnp.einsum('bqk,bvd->bqd', att, v)
        y = jnp.einsum('bqd,ed->bqe', y, w_fc) + b_fc
        h = x + y
        mu = jnp.mean(h, axis=-1, keepdims=True)
        var = jnp.var(h, axis=-1, keepdims=True)
        return (h - mu) * jax.lax.rsqrt(var + LN_EPS) * gamma + beta

    def _L0_ffn_ref(x, n1_w, n2_w, wq, wk, wv, wo, qn_w, kn_w, gate_w, e0_up, e0_down, e1_w1, e1_w2, e1_down, e2_l1, e2_l2, e2_l3, e2_l4, e3_down, e3_up, e3_out):
        import jax, jax.numpy as jnp
        import numpy as np
        DIM = 128
        HEADS = 16
        HD = DIM // HEADS
        M = 32
        E = 4
        K = 2
        HID = 256
        MID = 256
        LB = 0.01
        EPS = 1.1920929e-07

        def _rms(x, w):
            return x * jax.lax.rsqrt(jnp.mean(x * x, axis=-1, keepdims=True) + EPS) * w

        def _gelu(x):
            return jax.nn.gelu(x, approximate=False)
        B, T, C = x.shape
        h = _rms(x, n1_w)
        heads = lambda w_: (h @ w_.T).reshape(B, T, HEADS, HD).transpose(0, 2, 1, 3)
        q = _rms(heads(wq), qn_w)
        k = _rms(heads(wk), kn_w)
        v = heads(wv)
        scores = jnp.einsum('bhqd,bhkd->bhqk', q, k) * HD ** (-0.5)
        causal = jnp.tril(jnp.ones((T, T), bool))
        scores = jnp.where(causal[None, None], scores, -jnp.inf)
        attn = jax.nn.softmax(scores, axis=-1)
        ao = jnp.einsum('bhqk,bhkd->bhqd', attn, v).transpose(0, 2, 1, 3).reshape(B, T, C) @ wo.T
        ao = ao.at[:, :, :M].set(0.0)
        x = x + ao
        xf = _rms(x, n2_w).reshape(-1, C)
        N = xf.shape[0]
        logits = jnp.nan_to_num(xf @ gate_w.T)
        probs = jax.nn.softmax(logits, axis=-1)
        topv, topi = jax.lax.top_k(probs, K)
        topv = topv / (topv.sum(-1, keepdims=True) + 1e-08)
        wts = jnp.zeros((N, E), x.dtype).at[jnp.arange(N)[:, None], topi].add(topv)
        o0 = _gelu(xf @ e0_up.T) @ e0_down.T
        o1 = jax.nn.silu(xf @ e1_w1.T) * (xf @ e1_w2.T) @ e1_down.T
        o2 = _gelu(_gelu(_gelu(xf @ e2_l1.T) @ e2_l2.T) @ e2_l3.T) @ e2_l4.T
        o3 = _gelu(_gelu(xf @ e3_down.T) @ e3_up.T) @ e3_out.T
        moe = wts[:, 0:1] * o0 + wts[:, 1:2] * o1 + wts[:, 2:3] * o2 + wts[:, 3:4] * o3
        moe = moe.reshape(B, T, C).at[:, :, :M].set(0.0)
        return x + moe
    x = L0_attn_x
    xn = _layernorm(x, axis=-1)
    x = x + _L0_attn_ref(xn, L0_attn_w_qkv, L0_attn_w_fc, L0_attn_b_fc, L0_attn_gamma, L0_attn_beta) + _L0_ffn_ref(xn, L0_ffn_n1_w, L0_ffn_n2_w, L0_ffn_wq, L0_ffn_wk, L0_ffn_wv, L0_ffn_wo, L0_ffn_qn_w, L0_ffn_kn_w, L0_ffn_gate_w, L0_ffn_e0_up, L0_ffn_e0_down, L0_ffn_e1_w1, L0_ffn_e1_w2, L0_ffn_e1_down, L0_ffn_e2_l1, L0_ffn_e2_l2, L0_ffn_e2_l3, L0_ffn_e2_l4, L0_ffn_e3_down, L0_ffn_e3_up, L0_ffn_e3_out)
    return x

_drawn_inputs = setup_inputs


def setup_inputs(seed=0):
    import zlib

    import numpy as np

    out = dict(_drawn_inputs(seed))
    spreads = {'L0_attn_b_fc': (0.0, 2.0),
     'L0_attn_gamma': (1.0, 0.588),
     'L0_attn_beta': (0.0, 0.736),
     'L0_ffn_n1_w': (1.0, 0.6),
     'L0_ffn_n2_w': (1.0, 0.6),
     'L0_ffn_qn_w': (1.0, 0.6),
     'L0_ffn_kn_w': (1.0, 0.6)}
    factors = {'L0_ffn_wq': 8.0,
     'L0_ffn_wk': 8.0,
     'L0_ffn_wv': 8.0,
     'L0_ffn_wo': 8.0,
     'L0_ffn_gate_w': 8.0,
     'L0_ffn_e0_up': 8.0,
     'L0_ffn_e0_down': 8.0,
     'L0_ffn_e1_w1': 8.0,
     'L0_ffn_e1_w2': 8.0,
     'L0_ffn_e1_down': 8.0,
     'L0_ffn_e2_l1': 8.0,
     'L0_ffn_e2_l2': 8.0,
     'L0_ffn_e2_l3': 8.0,
     'L0_ffn_e2_l4': 8.0,
     'L0_ffn_e3_down': 8.0,
     'L0_ffn_e3_up': 8.0,
     'L0_ffn_e3_out': 8.0}
    for name, (base, spread) in spreads.items():
        noise = np.random.default_rng([zlib.crc32(name.encode()), seed]).standard_normal(out[name].shape)
        drawn = base * np.exp(spread * noise) if base else spread * noise
        out[name] = jnp.asarray(drawn.astype(out[name].dtype))
    for name, factor in factors.items():
        out[name] = (out[name] * factor).astype(out[name].dtype)
    return out
```

```python
from contextlib import ExitStack

import concourse.bass as bass
from concourse import mybir

ALU = mybir.AluOpType
ACT = mybir.ActivationFunctionType
F32 = mybir.dt.float32
F32R = mybir.dt.float32r
I32 = mybir.dt.int32
AX_X = mybir.AxisListType.X

P = 128
FLOAT_MAX = 3.4028234663852886e38
EXP_SAFE = 60.0
RSQRT_SEED = 0x5F3759DF

XT, QKV0, QKV1, Q0T, QT01, QT23, KT01, KT23, A_FILLS = range(9)
S00, S01, FC, OT0, OT1, AOT, WO, XFT, GATE, B_FILLS = range(10)
E1A, L1, L2, L3, EVEN_FILLS = range(5)
E1B, D3, U3, E0, ODD_FILLS = range(5)


def fused_block(nc: bass.Bass, x, w_qkv, w_fc, b_fc, gamma, beta, n1_w, n2_w, wq, wk, wv, wo, qn_w, kn_w,
                gate_w, e0_up, e0_down, e1_w1, e1_w2, e1_down, e2_l1, e2_l2, e2_l3, e2_l4, e3_down, e3_up,
                e3_out, out):
    BATCHES, SEQ, D = x.shape
    HD = qn_w.shape[0]
    HEADS = D // HD
    EXPERTS = gate_w.shape[0]
    HID = e0_up.shape[0]
    MASKED = 32
    KEPT = D - MASKED
    LN_EPS, RMS_EPS = 1e-5, 1.1920929e-07
    TILES = SEQ // P
    HC = HID // P
    LANES = 4
    GROUPS = HEADS // LANES
    UNITS = 3 * GROUPS
    SHIFT = 3 * HD
    assert D == P and TILES == 2 and HC == 2 and HD == 8 and BATCHES % 2 == 0

    with ExitStack() as ctx:
        def sb(name, shape, dt=F32):
            return ctx.enter_context(nc.sbuf_tensor(name, shape, dt))

        def psum(name):
            return ctx.enter_context(nc.psum_tensor(name, [P, 512], F32))

        def sem(name):
            return ctx.enter_context(nc.semaphore(name))

        scores_ps = [psum("scores0_ps"), psum("scores1_ps")]
        pv_ps = psum("pv_ps")
        even_ps, odd_ps = psum("even_ps"), psum("odd_ps")
        a_ps, b_ps, down_ps = psum("a_ps"), psum("b_ps"), psum("down_ps")
        setup_ps = [scores_ps[0], scores_ps[1], even_ps, odd_ps]

        nat_qkv0 = sb("nat_qkv0", [P, 3, D])
        nat_fc, nat_wo = sb("nat_fc", [P, D]), sb("nat_wo", [P, D])
        nat_q, nat_k, nat_v = sb("nat_q", [P, D]), sb("nat_k", [P, D]), sb("nat_v", [P, D])
        nat_gate = sb("nat_gate", [EXPERTS, D])
        nat_up = {n: sb(f"nat_{n}", [P, HC, D]) for n in ("e0u", "e1a", "e1b", "l1", "e3u")}
        nat_sq = {n: sb(f"nat_{n}", [P, HC, HID]) for n in ("l2", "l3")}
        nat_dn = {n: sb(f"nat_{n}", [P, HID]) for n in ("e0d", "e1d", "l4", "e3o")}
        nat_e3d = sb("nat_e3d", [P, D])

        qkvT = sb("qkvT", [P, 3 * D])
        m0 = sb("m0", [P, D])
        fcwoT = sb("fcwoT", [P, 2 * D])
        vfc = sb("vfc", [P, D])
        e1T = sb("e1T", [P, 2 * HID])
        l1T = sb("l1T", [P, HID + D + EXPERTS])
        e0uT = sb("e0uT", [P, HID])
        l2T, l3T = sb("l2T", [P, HC * HID]), sb("l3T", [P, HC * HID])
        e3u_l4T = sb("e3u_l4T", [P, 2 * HID])
        e0d_e1dT = sb("e0d_e1dT", [P, 2 * HID])
        e3oT = sb("e3oT", [P, HID])
        fcT, woT = fcwoT[:, 0:D], fcwoT[:, D:2 * D]
        e3dT, gateT = l1T[:, HID:HID + D], l1T[:, HID + D:HID + D + EXPERTS]
        downT = [e0d_e1dT[:, 0:HID], e0d_e1dT[:, HID:2 * HID], e3u_l4T[:, HID:2 * HID], e3oT[:, :]]

        ident = sb("ident", [P, P])
        n1_col, n2_col = sb("n1_col", [P, 1]), sb("n2_col", [P, 1])
        qn_row, kn_row, qk_w = sb("qn_row", [P, HD]), sb("kn_row", [P, HD]), sb("qk_w", [P, HD])
        bfc_row, gamma_row, beta_row = sb("bfc_row", [P, D]), sb("gamma_row", [P, D]), sb("beta_row", [P, D])
        minus_half = sb("minus_half", [P, TILES])
        lower = sb("lower", [P, EXPERTS, EXPERTS])
        ones = sb("ones", [P, P])
        widest, bounded = sb("widest", [1, 1]), sb("bounded", [1, 1], I32)
        mx_sb = sb("mx_sb", [P, LANES, P])
        mx = sb("mx", [P, TILES, TILES, HEADS])

        x_sb = [sb(f"x_sb{p}", [P, TILES, D]) for p in range(2)]
        ln_st = sb("ln_st", [P, TILES, 6])
        ln_mv = sb("ln_mv", [P, TILES, 2])
        ln_rstd, h_scale, ln_tmp = sb("ln_rstd", [P, TILES]), sb("h_scale", [P, TILES]), sb("ln_tmp", [P, TILES])
        xn = [sb(f"xn{p}", [P, TILES, D]) for p in range(2)]
        xnT = [sb(f"xnT{p}", [P, SEQ]) for p in range(2)]
        xn_sum = [sb(f"xn_sum{p}", [P, 1]) for p in range(2)]
        q0T = [sb(f"q0T{p}", [P, SEQ]) for p in range(2)]
        qkv = sb("qkv", [P, TILES, 3 * D])
        qk_sq = sb("qk_sq", [P, TILES, 2 * D])
        qk_ms = sb("qk_ms", [P, TILES, 2 * HEADS])
        qk_y, qk_t = sb("qk_y", [P, TILES, 2 * HEADS]), sb("qk_t", [P, TILES, 2 * HEADS])
        qk_n = sb("qk_n", [P, TILES, 2 * HEADS, HD])
        qk_parts = sb("qk_parts", [P, TILES, 2 * HEADS, 32], F32R)
        v_aug = [sb(f"v_aug{p}", [P, TILES, HEADS, 32]) for p in range(2)]
        qT = [sb(f"qT{p}", [P, GROUPS, SEQ], F32R) for p in range(2)]
        kT = sb("kT", [P, GROUPS, SEQ], F32R)
        k_lane = [sb(f"k_lane{p}", [P, LANES, GROUPS, SEQ], F32R) for p in range(2)]

        probs = [sb(f"probs{g}", [P, LANES, SEQ + P]) for g in range(2)]
        pvT = sb("pvT", [P, GROUPS, SEQ])
        row_inv = sb("row_inv", [P, HEADS])
        ao = sb("ao", [P, TILES, D])
        aoT = sb("aoT", [P, SEQ])
        a0_negmax, a0_sum = sb("a0_negmax", [P, TILES]), sb("a0_sum", [P, TILES])
        a0_inv, a0_row = sb("a0_inv", [P, TILES]), sb("a0_row", [P, TILES])
        a0_exp = sb("a0_exp", [P, SEQ])
        xsum_cols = sb("xsum_cols", [P, P])
        xn_b = sb("xn_b", [P, TILES, D])
        h0, h0n = sb("h0", [P, TILES, D]), sb("h0n", [P, TILES, D])
        h0_st, h0_mv = sb("h0_st", [P, TILES, 6]), sb("h0_mv", [P, TILES, 2])
        h0_rstd = sb("h0_rstd", [P, TILES])
        x1 = sb("x1_sb", [P, TILES, D])
        x1_ms, x1_scale = sb("x1_ms", [P, TILES]), sb("x1_scale", [P, TILES])
        x1_sq = sb("x1_sq", [P, D])
        xf = sb("xf", [P, TILES, D])
        xfT = [sb(f"xfT{p}", [P, SEQ]) for p in range(2)]
        acc = [sb(f"acc{p}", [P, TILES, D]) for p in range(2)]
        logits = [sb(f"logits{p}", [P, TILES, EXPERTS]) for p in range(2)]

        g_a, g_b, g_c = (sb(f"gate_{n}", [P, TILES, EXPERTS]) for n in "abc")
        g_m = sb("gate_m", [P, TILES])
        g_gt, g_eq = sb("gate_gt", [P, TILES, EXPERTS, EXPERTS]), sb("gate_eq", [P, TILES, EXPERTS, EXPERTS])
        wts = sb("wts", [P, TILES, EXPERTS])
        e1_t, e1_s, e1_h = (sb(f"e1_{n}", [P, HC, SEQ]) for n in "tsh")
        l1_h, l2_h, l3_h = sb("l1_h", [P, HC, SEQ]), sb("l2_h", [P, HC, SEQ]), sb("l3_h", [P, HC, SEQ])
        d3_h, u3_h, e0_h = sb("d3_h", [P, SEQ]), sb("u3_h", [P, HC, SEQ]), sb("e0_h", [P, HC, SEQ])
        hidden = [e0_h, e1_h, l3_h, u3_h]

        names = """ident_ready consts_ready w_attn_in w_up_in w_sq_in w_dn_in rows_in
                   setup_full setup_dve setup_act qk_w_ready zeros_ready flag_ready
                   mx_full mx_copied mx_masked mx_reduced mx_shifted mx_turned mx_back mx_reset
                   ln_stats ln_scaled xn_ready a_full a_read qk_split v_ready
                   scores_full exp_done probs_masked pv_full pv_read
                   b_full b_read a0_maxed a0_rowed xsum_ready h0_stats h0_scaled h0_normed
                   xnb_ready x1_started x1_squared x1_scaled xf_ready acc_ready
                   gate_shifted gate_exped wts_ready e1_tanh
                   even_full even_read odd_full odd_read down_full down_read
                   dve_a dve_b dve_c dve_d dve_l dve_s pool_l pool_b pool_s""".split()
        s = {n: sem(n) for n in names}
        x_in, k_in, acc_in, out_done = ([sem(f"{n}{p}") for p in range(2)] for n in ("x_in", "k_in", "acc_in", "out_done"))

        DVE_A, DVE_B, DVE_C, DVE_D, DVE_L, POOL_L, POOL_B = 19, 4, 15, 6, 1, 5, 3
        ROUNDS = GROUPS * (TILES * (TILES + 1) // 2)

        ROUND_LIST = [(j, g, kt) for j in range(TILES) for g in range(GROUPS) for kt in range(j + 1)]

        block = ctx.enter_context(nc.Block())

        def wait(eng, name, value):
            if not isinstance(value, int) or value > 0:
                eng.wait_ge(s[name] if isinstance(name, str) else name, value)

        def pipeline(slot):
            slot((0, 0), None, None, None)
            slot((0, 1), (0, 0), None, None)
            slot((1, 0), (0, 1), (0, 0), None)
            for n in range(BATCHES // 2 - 2):
                slot((n + 1, 1), (n + 1, 0), (n, 1), (n, 0))
                slot((n + 2, 0), (n + 1, 1), (n + 1, 0), (n, 1))
            last = BATCHES // 2 - 1
            slot((last, 1), (last, 0), (last - 1, 1), (last - 1, 0))
            slot(None, (last, 1), (last, 0), (last - 1, 1))
            slot(None, None, (last, 1), (last, 0))
            slot(None, None, None, (last, 1))

        def number(batch):
            return 2 * batch[0] + batch[1]

        @block.sync
        def _(sp):
            sp.dma_start(x_sb[0][:], x[0].rearrange("(j p) d -> p j d", p=P)).then_inc(x_in[0], 16)
            sp.dma_start(nat_qkv0[:], w_qkv.rearrange("(c p) d -> p c d", p=P)).then_inc(s["w_attn_in"], 16)
            for dst, src in ((nat_q, wq), (nat_k, wk), (nat_v, wv), (nat_fc, w_fc), (nat_wo, wo)):
                sp.dma_start(dst[:], src).then_inc(s["w_attn_in"], 16)
            sp.dma_start(x_sb[1][:], x[1].rearrange("(j p) d -> p j d", p=P)).then_inc(x_in[1], 16)
            for name, src in (("l2", e2_l2), ("l3", e2_l3)):
                sp.dma_start(nat_sq[name][:], src.rearrange("(c p) d -> p c d", p=P)).then_inc(s["w_sq_in"], 16)

            def rows_of(t, batch):
                return t[batch].rearrange("(j p) d -> p j d", p=P)

            def slot(L, A, B, C):
                if L is not None and L[0] != 0:
                    n, p = L
                    wait(sp, "xn_ready", number(L) - 1)
                    sp.dma_start(x_sb[p][:], rows_of(x, number(L))).then_inc(x_in[p], 16)
                if B is not None:
                    n, p = B
                    wait(sp, out_done[p], 16 * n)
                    sp.dma_start(acc[p][:], rows_of(x, number(B))).then_inc(acc_in[p], 16)
                if A is not None:
                    n, p = A
                    a = number(A)
                    wait(sp, "a_read", A_FILLS * a + KT23 + 1)
                    wait(sp, "scores_full", UNITS * (a - 1))
                    for lane in range(LANES):
                        rows = slice(32 * lane, 32 * lane + 32)
                        sp.dma_start(k_lane[p][rows, lane].bitcast(F32), kT[rows].bitcast(F32)).then_inc(k_in[p], 16)
                if C is not None:
                    n, p = C
                    wait(sp, "down_read", TILES * number(C) + TILES)
                    sp.dma_start(rows_of(out, number(C)), acc[p][:]).then_inc(out_done[p], 16)

            pipeline(slot)
            for p in range(2):
                sp.wait_ge(out_done[p], 16 * (BATCHES // 2))

        @block.gpsimd
        def _(pool):
            def step(ins, name, value):
                ins.then_inc(s[name], 1)
                pool.wait_ge(s[name], value)

            step(nc.gpsimd.memset(ident[:], 0.0), "pool_s", 1)
            nc.gpsimd.affine_select(out=ident[:], in_=ident[:], compare_op=ALU.not_equal, fill=1.0, base=0,
                                    pattern=[[-1, P]], channel_multiplier=1).then_inc(s["ident_ready"], 1)
            nc.gpsimd.memset(minus_half[:], -0.5)
            nc.gpsimd.memset(ones[:], 1.0)
            step(nc.gpsimd.memset(qk_parts[:].bitcast(F32), 0.0), "pool_s", 2)
            nc.gpsimd.memset(qk_parts[:, :, HEADS:, SHIFT:SHIFT + 1].bitcast(F32), 1.0)
            step(nc.gpsimd.memset(lower[:], 1.0), "pool_s", 3)
            nc.gpsimd.affine_select(out=lower[:], in_=lower[:], compare_op=ALU.is_gt, fill=0.0, base=0,
                                    pattern=[[1, EXPERTS], [-1, EXPERTS]], channel_multiplier=0
                                    ).then_inc(s["consts_ready"], 1)
            for p in range(2):
                step(nc.gpsimd.memset(v_aug[p][:], 0.0), "pool_s", 4 + p)
                nc.gpsimd.memset(v_aug[p][:, :, :, HD:HD + 1], 1.0).then_inc(s["zeros_ready"], 1)
            pool.wait_ge(s["consts_ready"], 1)
            pool.wait_ge(s["zeros_ready"], 2)
            pool.wait_ge(s["flag_ready"], 1)
            needs_max = pool.value_load(bounded[0:1, 0:1], min_val=0, max_val=1) == 0

            def slot(L, A, B, C):
                def mask_probs(g):
                    if B is None:
                        return
                    b = number(B)
                    buf = probs[g % 2]
                    for part, units in ((buf[:, :, 0:P], 2), (buf[:, :, SEQ:SEQ + P], 3)):
                        wait(pool, "exp_done", UNITS * b + 3 * g + units)
                        nc.gpsimd.affine_select(out=part, in_=part, compare_op=ALU.is_ge, fill=0.0, base=0,
                                                pattern=[[0, LANES], [1, P]], channel_multiplier=-1
                                                ).then_inc(s["probs_masked"], 1)

                if B is not None:
                    n, p = B
                    b = number(B)
                    wait(pool, "xn_ready", b + 1)
                    wait(pool, "b_read", B_FILLS * (b - 1) + FC + 1)
                    nc.gpsimd.tensor_tensor(xn_b[:], xn[p][:], bfc_row[:].unsqueeze(1).to_broadcast([P, TILES, D]),
                                            ALU.add).then_inc(s["xnb_ready"], 1)
                    wait(pool, "acc_ready", b)
                    wait(pool, "xf_ready", b)
                    nc.gpsimd.tensor_copy(x1[:], xn[p][:]).then_inc(s["x1_started"], 1)
                mask_probs(0)
                mask_probs(1)
                mask_probs(2)
                mask_probs(3)
                if A is not None:
                    n, p = A
                    a = number(A)
                    wait(pool, "a_read", A_FILLS * a + QKV1 + 1)
                    wait(pool, "pv_full", GROUPS * (a - 1))
                    nc.gpsimd.tensor_copy(v_aug[p][:, :, :, 0:HD],
                                          qkv[:, :, 2 * D:3 * D].rearrange("p j (h e) -> p j h e", e=HD)
                                          ).then_inc(s["v_ready"], 1)
                if B is not None:
                    n, p = B
                    b = number(B)
                    k = [POOL_B * b]

                    def step_b(ins):
                        k[0] += 1
                        ins.then_inc(s["pool_b"], 1)
                        pool.wait_ge(s["pool_b"], k[0])

                    wait(pool, "h0_stats", b + 1)
                    nc.gpsimd.tensor_scalar(h0_rstd[:], h0_mv[:, :, 1], LN_EPS, 1.0, ALU.add, ALU.mult
                                            ).then_inc(s["h0_scaled"], 1)
                    pool.wait_ge(s["h0_scaled"], 2 * b + 1)
                    nc.gpsimd.tensor_tensor(h0_rstd[:], h0_rstd[:], minus_half[:], ALU.pow
                                            ).then_inc(s["h0_scaled"], 1)
                    wait(pool, "h0_normed", b + 1)
                    pool.wait_ge(acc_in[p], 16 * (n + 1))
                    step_b(nc.gpsimd.tensor_tensor(h0n[:], h0n[:], gamma_row[:].unsqueeze(1).to_broadcast([P, TILES, D]),
                                                   ALU.mult))
                    step_b(nc.gpsimd.tensor_tensor(h0n[:], h0n[:], beta_row[:].unsqueeze(1).to_broadcast([P, TILES, D]),
                                                   ALU.add))
                    step_b(nc.gpsimd.tensor_tensor(acc[p][:], h0n[:], acc[p][:], ALU.add))
                    wait(pool, "x1_squared", TILES * b + TILES)
                    nc.gpsimd.tensor_scalar(x1_scale[:], x1_ms[:], RMS_EPS, 1.0, ALU.add, ALU.mult
                                            ).then_inc(s["x1_scaled"], 1)
                    pool.wait_ge(s["x1_scaled"], 2 * b + 1)
                    nc.gpsimd.tensor_tensor(x1_scale[:], x1_scale[:], minus_half[:], ALU.pow
                                            ).then_inc(s["x1_scaled"], 1)
                    wait(pool, "b_read", B_FILLS * b + WO + 1)
                    nc.gpsimd.tensor_tensor(acc[p][:], acc[p][:], x1[:], ALU.add).then_inc(s["acc_ready"], 1)
                if L is not None:
                    l = number(L)
                    k_l = [POOL_L * l]

                    def step_l(ins):
                        k_l[0] += 1
                        ins.then_inc(s["pool_l"], 1)
                        pool.wait_ge(s["pool_l"], k_l[0])

                    wait(pool, "ln_stats", l + 1)
                    wait(pool, "a_read", A_FILLS * (l - 1) + QKV1 + 1)
                    var = ln_mv[:, :, 1]
                    step_l(nc.gpsimd.tensor_scalar(ln_tmp[:], var, LN_EPS, 1.0, ALU.add, ALU.mult))
                    step_l(nc.gpsimd.tensor_tensor(ln_rstd[:], ln_tmp[:], minus_half[:], ALU.pow))
                    step_l(nc.gpsimd.tensor_tensor(ln_tmp[:], ln_rstd[:], ln_rstd[:], ALU.mult))
                    step_l(nc.gpsimd.tensor_tensor(ln_tmp[:], ln_tmp[:], var, ALU.mult))
                    step_l(nc.gpsimd.tensor_scalar(ln_tmp[:], ln_tmp[:], RMS_EPS, 1.0, ALU.add, ALU.mult))
                    nc.gpsimd.tensor_tensor(h_scale[:], ln_tmp[:], minus_half[:], ALU.pow
                                            ).then_inc(s["ln_scaled"], 1)
                if A is not None:
                    with pool.If(needs_max):
                        a = number(A)
                        for r, (j, g, kt) in enumerate(ROUND_LIST):
                            if kt == j:
                                wait(pool, "mx_copied", ROUNDS * a + r + 1)
                                nc.gpsimd.affine_select(out=mx_sb[:], in_=mx_sb[:], compare_op=ALU.is_ge, fill=-FLOAT_MAX,
                                                        base=0, pattern=[[0, LANES], [-1, P]], channel_multiplier=1
                                                        ).then_inc(s["mx_masked"], 1)

            pipeline(slot)

        @block.scalar
        def _(act):
            for dst, src in ((n1_col, n1_w), (n2_col, n2_w)):
                act.dma_start(dst[:], src.rearrange("(p a) -> p a", a=1)).then_inc(s["rows_in"], 16)
            for dst, src in ((qn_row, qn_w), (kn_row, kn_w), (bfc_row, b_fc), (gamma_row, gamma), (beta_row, beta)):
                act.dma_start(dst[:], src.partition_broadcast(P)).then_inc(s["rows_in"], 16)
            for name, src in (("e1a", e1_w1), ("e1b", e1_w2), ("l1", e2_l1), ("e0u", e0_up), ("e3u", e3_up)):
                act.dma_start(nat_up[name][:], src.rearrange("(c p) d -> p c d", p=P)).then_inc(s["w_up_in"], 16)
            act.dma_start(nat_e3d[:], e3_down).then_inc(s["w_up_in"], 16)
            act.dma_start(nat_gate[:], gate_w).then_inc(s["w_up_in"], 16)
            for name, src in (("e0d", e0_down), ("e1d", e1_down), ("l4", e2_l4), ("e3o", e3_out)):
                act.dma_start(nat_dn[name][:], src).then_inc(s["w_dn_in"], 16)

            act.wait_ge(s["rows_in"], 7 * 16)
            for f, (dst, scale) in enumerate(((m0, float(D) ** -0.5), (vfc, 1.0), (l1T, n2_col[:, 0:1]), (l2T, 1.0),
                                              (e3u_l4T, 1.0), (e3oT, 1.0))):
                act.wait_ge(s["setup_full"], 2 * f + 2)
                nc.scalar.activation(dst[:], setup_ps[(2 * f + 1) % 4][:, 0:dst.shape[1]], ACT.Copy, scale=scale
                                     ).then_inc(s["setup_act"], 1)

            def slot(L, A, B, C):
                a, b, c = (number(t) if t is not None else None for t in (A, B, C))

                def exp_unit(u):
                    if B is None:
                        return
                    g, part = divmod(u, 3)
                    wait(act, "scores_full", UNITS * b + u + 1)
                    if part == 0:
                        wait(act, "pv_full", GROUPS * b + g - 1)
                    dst = (probs[g % 2][:, 0:2, 0:SEQ], probs[g % 2][:, 2:4, 0:SEQ], probs[g % 2][:, :, SEQ:SEQ + P])[part]
                    src = scores_ps[u % 2][:].rearrange("p (l q) -> p l q", q=dst.shape[2])
                    nc.scalar.activation(dst, src, ACT.Exp).then_inc(s["exp_done"], 1)

                def a0_softmax(j):
                    if B is None:
                        return
                    wait(act, "a0_maxed", TILES * b + j + 1)
                    if j == 0:
                        wait(act, "a0_rowed", b)
                    nc.scalar.activation(a0_exp[:], b_ps[:, 0:SEQ], ACT.Exp, bias=a0_negmax[:, j:j + 1],
                                         accum_out=a0_sum[:, j:j + 1]).then_inc(s["b_read"], 1)

                def x_copy():
                    if A is None:
                        return
                    p = A[1]
                    wait(act, "a_full", A_FILLS * a + XT + 1)
                    wait(act, "xsum_ready", a - 1)
                    wait(act, "b_full", B_FILLS * (a - 2) + S01 + 1)
                    nc.scalar.activation(xnT[p][:], a_ps[:, 0:SEQ], ACT.Copy, accum_out=xn_sum[p][:]
                                         ).then_inc(s["a_read"], 1)

                def q0_copy():
                    if A is None:
                        return
                    wait(act, "a_full", A_FILLS * a + Q0T + 1)
                    nc.scalar.copy(q0T[A[1]][:], a_ps[:, 0:SEQ]).then_inc(s["a_read"], 1)

                def qkv_copy(j):
                    if A is None:
                        return
                    wait(act, "a_full", A_FILLS * a + QKV0 + j + 1)
                    wait(act, "ln_scaled", a + 1)
                    wait(act, "v_ready", a)
                    wait(act, "qk_split", a)
                    nc.scalar.activation(qkv[:, j, :], a_ps[:, 0:3 * D], ACT.Copy, scale=h_scale[:, j:j + 1]
                                         ).then_inc(s["a_read"], 1)

                def e1_tanh():
                    if C is None:
                        return
                    wait(act, "even_full", EVEN_FILLS * c + E1A + 1)
                    wait(act, "odd_read", ODD_FILLS * c)
                    nc.scalar.activation(e1_t[:].rearrange("p c q -> p (c q)"), even_ps[:], ACT.Tanh, scale=0.5
                                         ).then_inc(s["e1_tanh"], 1)

                def gate_exp():
                    if C is None:
                        return
                    wait(act, "gate_shifted", c + 1)
                    nc.scalar.activation(g_b[:], g_a[:], ACT.Exp).then_inc(s["gate_exped"], 1)

                x_copy()
                exp_unit(0)
                exp_unit(1)
                qkv_copy(0)
                exp_unit(2)
                qkv_copy(1)
                exp_unit(3)
                e1_tanh()
                q0_copy()
                gate_exp()
                exp_unit(4)
                a0_softmax(0)
                exp_unit(5)
                exp_unit(6)
                exp_unit(7)
                a0_softmax(1)
                exp_unit(8)
                exp_unit(9)
                exp_unit(10)
                exp_unit(11)

                def gelu(full, fill, ps, dst, done):
                    if C is None:
                        return
                    wait(act, full, 4 * c + fill + 1)
                    ncol = dst.shape[1] * (dst.shape[2] if len(dst.shape) == 3 else 1)
                    flat = dst[:].rearrange("p c q -> p (c q)") if len(dst.shape) == 3 else dst[:]
                    nc.scalar.activation(flat, ps[:, 0:ncol], ACT.Gelu).then_inc(s[done], 1)

                gelu("even_full", L1, even_ps, l1_h, "even_read")
                gelu("odd_full", D3, odd_ps, d3_h, "odd_read")
                gelu("even_full", L2, even_ps, l2_h, "even_read")

                def qk_copy(fill, dst):
                    if A is None:
                        return
                    wait(act, "a_full", A_FILLS * a + fill + 1)
                    if fill == KT23:
                        wait(act, k_in[1 - A[1]], 16 * LANES * (A[0] + A[1]))
                    nc.scalar.copy(dst, a_ps[:].rearrange("p (g t) -> p g t", t=SEQ)).then_inc(s["a_read"], 1)

                gelu("odd_full", U3, odd_ps, u3_h, "odd_read")
                if B is not None:
                    wait(act, "b_full", B_FILLS * b + AOT + 1)
                    nc.scalar.copy(aoT[:], b_ps[:, 0:SEQ]).then_inc(s["b_read"], 1)
                if A is not None:
                    qk_copy(QT23, qT[A[1]][:, 2:4, :])
                gelu("even_full", L3, even_ps, l3_h, "even_read")
                if B is not None:
                    wait(act, "b_read", B_FILLS * b + WO + 1)
                    for j in range(TILES):
                        if j or not isinstance(b, int) or b:
                            wait(act, "x1_squared", TILES * b + j)
                        nc.scalar.activation(x1_sq[:], x1[:, j, :], ACT.Square, scale=float(D) ** -0.5,
                                             accum_out=x1_ms[:, j:j + 1]).then_inc(s["x1_squared"], 1)
                gelu("odd_full", E0, odd_ps, e0_h, "odd_read")
                if A is not None:
                    qk_copy(KT23, kT[:, 2:4, :])
                if B is not None:
                    wait(act, "b_full", B_FILLS * b + XFT + 1)
                    nc.scalar.copy(xfT[B[1]][:], b_ps[:, 0:SEQ]).then_inc(s["b_read"], 1)

            pipeline(slot)

        @block.vector
        def _(dve):
            V = nc.vector
            for p in range(2):
                V.memset(k_lane[p][:].bitcast(F32), 0.0).then_inc(s["zeros_ready"], 1)
            dve.wait_ge(s["rows_in"], 7 * 16)
            V.scalar_tensor_tensor(out=qk_w[:], in0=qn_row[:], scalar=float(HD) ** -0.5, in1=kn_row[:], op0=ALU.mult,
                                   op1=ALU.mult).then_inc(s["qk_w_ready"], 1)
            for f, (dst, scale) in enumerate(((qkvT, n1_col[:, 0:1]), (fcwoT, 1.0), (e1T, n2_col[:, 0:1]),
                                              (e0uT, n2_col[:, 0:1]), (l3T, 1.0), (e0d_e1dT, 1.0))):
                dve.wait_ge(s["setup_full"], 2 * f + 1)
                V.tensor_scalar(dst[:], setup_ps[(2 * f) % 4][:, 0:dst.shape[1]], scale, None, ALU.mult
                                ).then_inc(s["setup_dve"], 1)
            dve.wait_ge(s["qk_w_ready"], 1)
            V.tensor_reduce(widest[:], qk_w[0:1, :], AX_X, ALU.max, apply_absolute_value=True).then_inc(s["dve_s"], 1)
            dve.wait_ge(s["dve_s"], 1)
            V.tensor_scalar(bounded[:], widest[:], EXP_SAFE / HD, None, ALU.is_le).then_inc(s["flag_ready"], 1)
            dve.wait_ge(s["flag_ready"], 1)
            needs_max = dve.value_load(bounded[0:1, 0:1], min_val=0, max_val=1) == 0
            dve.wait_ge(s["consts_ready"], 1)

            def slot(L, A, B, C):
                l, a, b, c = (number(t) if t is not None else None for t in (L, A, B, C))
                count = {}

                def step(ins, name, batch, per_batch):
                    count[name] = count.get(name, 0) + 1
                    assert count[name] <= per_batch, name
                    ins.then_inc(s[name], 1)
                    dve.wait_ge(s[name], batch * per_batch + count[name])

                def step_a(ins):
                    step(ins, "dve_a", a, DVE_A)

                def step_l(ins):
                    step(ins, "dve_l", l, DVE_L)

                def step_b(ins):
                    step(ins, "dve_b", b, DVE_B)

                def step_c(ins):
                    step(ins, "dve_c", c, DVE_C)

                def step_d(ins):
                    step(ins, "dve_d", c, DVE_D)

                def gate_scores():
                    if C is None:
                        return
                    lg = logits[C[1]]
                    wait(dve, "gate_exped", c)
                    wait(dve, "b_read", B_FILLS * (c + 1))
                    V.tensor_scalar(g_a[:], lg[:], FLOAT_MAX, -FLOAT_MAX, ALU.min, ALU.max)
                    step_c(V.tensor_tensor(g_c[:], lg[:], lg[:], ALU.is_equal))
                    step_c(V.tensor_tensor(g_a[:], g_a[:], g_c[:], ALU.mult))
                    step_c(V.tensor_reduce(g_m[:], g_a[:], AX_X, ALU.max))
                    V.tensor_tensor(g_a[:], g_a[:], g_m[:].unsqueeze(2).to_broadcast([P, TILES, EXPERTS]),
                                    ALU.subtract).then_inc(s["gate_shifted"], 1)

                def gate_weights():
                    if C is None:
                        return
                    wait(dve, "gate_exped", c + 1)
                    step_c(V.tensor_reduce(g_m[:], g_b[:], AX_X, ALU.add))
                    step_c(V.reciprocal(g_m[:], g_m[:]))
                    step_c(V.tensor_tensor(g_b[:], g_b[:], g_m[:].unsqueeze(2).to_broadcast([P, TILES, EXPERTS]),
                                           ALU.mult))
                    for j in range(TILES):
                        other = g_b[:, j, :].unsqueeze(1).to_broadcast([P, EXPERTS, EXPERTS])
                        own = g_b[:, j, :].unsqueeze(2).to_broadcast([P, EXPERTS, EXPERTS])
                        V.tensor_tensor(g_eq[:, j], other, own, ALU.is_equal)
                        ins = V.tensor_tensor(g_gt[:, j], other, own, ALU.is_gt)
                    step_c(ins)
                    for j in range(TILES):
                        ins = V.tensor_tensor(g_eq[:, j], g_eq[:, j], lower[:], ALU.mult)
                    step_c(ins)
                    step_c(V.tensor_tensor(g_gt[:], g_gt[:], g_eq[:], ALU.add))
                    step_c(V.tensor_reduce(g_c[:], g_gt[:], AX_X, ALU.add))
                    step_c(V.scalar_tensor_tensor(out=g_c[:], in0=g_c[:], scalar=2.0, in1=g_b[:], op0=ALU.is_lt,
                                                  op1=ALU.mult))
                    step_c(V.tensor_reduce(g_m[:], g_c[:], AX_X, ALU.add))
                    step_c(V.tensor_scalar(g_m[:], g_m[:], 1e-8, None, ALU.add))
                    step_c(V.reciprocal(g_m[:], g_m[:]))
                    step_c(V.tensor_tensor(wts[:], g_c[:], g_m[:].unsqueeze(2).to_broadcast([P, TILES, EXPERTS]),
                                           ALU.mult))
                    assert count["dve_c"] == DVE_C, count

                def e1_gate():
                    if C is None:
                        return
                    wait(dve, "e1_tanh", c + 1)
                    V.scalar_tensor_tensor(out=e1_s[:].rearrange("p c q -> p (c q)"), in0=e1_t[:].rearrange("p c q -> p (c q)"),
                                           scalar=1.0, in1=even_ps[:], op0=ALU.add, op1=ALU.mult
                                           ).then_inc(s["even_read"], 1)

                def e1_product():
                    if C is None:
                        return
                    wait(dve, "even_read", EVEN_FILLS * c + E1A + 1)
                    wait(dve, "odd_full", ODD_FILLS * c + E1B + 1)
                    V.scalar_tensor_tensor(out=e1_h[:].rearrange("p c q -> p (c q)"), in0=e1_s[:].rearrange("p c q -> p (c q)"),
                                           scalar=0.5, in1=odd_ps[:], op0=ALU.mult, op1=ALU.mult
                                           ).then_inc(s["odd_read"], 1)

                def pv_copy(g):
                    if B is None:
                        return
                    wait(dve, "pv_full", GROUPS * b + g + 1)
                    if g == 0:
                        wait(dve, "b_full", B_FILLS * (b - 1) + OT1 + 1)
                    V.tensor_copy(pvT[:, g, :], pv_ps[:, 0:SEQ]).then_inc(s["pv_read"], 1)

                def qk_square(j):
                    if A is None:
                        return
                    wait(dve, "a_read", A_FILLS * a + QKV0 + j + 1)
                    step_a(V.tensor_tensor(qk_sq[:, j, :], qkv[:, j, 0:2 * D], qkv[:, j, 0:2 * D], ALU.mult))
                    step_a(V.tensor_reduce(qk_ms[:, j, :], qk_sq[:, j, :].rearrange("p (h e) -> p h e", e=HD), AX_X,
                                           ALU.add))

                def rsqrt_guess():
                    if A is None:
                        return
                    step_a(V.tensor_scalar(qk_ms[:], qk_ms[:], 1.0 / HD, RMS_EPS, ALU.mult, ALU.add))
                    step_a(V.tensor_scalar(qk_t[:].bitcast(I32), qk_ms[:].bitcast(I32), 1, None, ALU.logical_shift_right))
                    step_a(V.tensor_scalar(qk_y[:].bitcast(I32), qk_t[:].bitcast(I32), -1.0, float(RSQRT_SEED), ALU.mult,
                                           ALU.add))

                def rsqrt_newton():
                    if A is None:
                        return
                    step_a(V.tensor_tensor(qk_t[:], qk_y[:], qk_y[:], ALU.mult))
                    step_a(V.scalar_tensor_tensor(out=qk_t[:], in0=qk_t[:], scalar=-0.5, in1=qk_ms[:], op0=ALU.mult,
                                                  op1=ALU.mult))
                    step_a(V.scalar_tensor_tensor(out=qk_y[:], in0=qk_t[:], scalar=1.5, in1=qk_y[:], op0=ALU.add,
                                                  op1=ALU.mult))

                def qk_norm_split():
                    if A is None:
                        return
                    for j in range(TILES):
                        ins = V.tensor_tensor(qk_n[:, j], qkv[:, j, 0:2 * D].rearrange("p (h e) -> p h e", e=HD),
                                              qk_y[:, j].unsqueeze(2).to_broadcast([P, 2 * HEADS, HD]), ALU.mult)
                    step_a(ins)
                    for j in range(TILES):
                        ins = V.tensor_tensor(qk_n[:, j, 0:HEADS, :], qk_n[:, j, 0:HEADS, :],
                                              qk_w[:].unsqueeze(1).to_broadcast([P, HEADS, HD]), ALU.mult)
                    step_a(ins)
                    wait(dve, "a_full", A_FILLS * a)
                    for j in range(TILES):
                        ins = V.tensor_copy(qk_parts[:, j, :, 0:HD], qk_n[:, j])
                    step_a(ins)
                    for j in range(TILES):
                        V.tensor_tensor(qk_parts[:, j, 0:HEADS, 2 * HD:3 * HD], qk_n[:, j, 0:HEADS],
                                        qk_parts[:, j, 0:HEADS, 0:HD].bitcast(F32), ALU.subtract)
                        V.tensor_tensor(qk_parts[:, j, HEADS:, HD:2 * HD], qk_n[:, j, HEADS:],
                                        qk_parts[:, j, HEADS:, 0:HD].bitcast(F32), ALU.subtract)
                        V.tensor_copy(qk_parts[:, j, 0:HEADS, HD:2 * HD], qk_parts[:, j, 0:HEADS, 0:HD])
                        ins = V.tensor_copy(qk_parts[:, j, HEADS:, 2 * HD:3 * HD], qk_parts[:, j, HEADS:, 0:HD])
                    ins.then_inc(s["qk_split"], 1)

                def a0_max(j):
                    if B is None:
                        return
                    wait(dve, "b_full", B_FILLS * b + S00 + j + 1)
                    V.tensor_reduce(a0_negmax[:, j:j + 1], b_ps[:, 0:SEQ], AX_X, ALU.max, negate=True
                                    ).then_inc(s["a0_maxed"], 1)

                def a0_xsum():
                    if B is None:
                        return
                    wait(dve, "b_full", B_FILLS * (b - 1) + FC + 1)
                    V.tensor_scalar(xsum_cols[:], ones[:], xn_sum[B[1]][:, 0:1], None, ALU.mult).then_inc(s["xsum_ready"], 1)

                def a0_rows():
                    if B is None:
                        return
                    wait(dve, "b_read", B_FILLS * b + S01 + 1)
                    wait(dve, "h0_normed", b)
                    step_b(V.reciprocal(a0_inv[:], a0_sum[:]))
                    V.tensor_tensor(a0_row[:], a0_sum[:], a0_inv[:], ALU.mult).then_inc(s["a0_rowed"], 1)
                    wait(dve, "b_full", B_FILLS * b + FC + 1)
                    wait(dve, "xnb_ready", b + 1)
                    dve.wait_ge(s["a0_rowed"], b + 1)
                    for j in range(TILES):
                        ins = V.scalar_tensor_tensor(out=h0[:, j, :], in0=b_ps[:, 0:D], scalar=a0_row[:, j:j + 1],
                                                     in1=xn_b[:, j, :], op0=ALU.mult, op1=ALU.add)
                    ins.then_inc(s["b_read"], 1)
                    dve.wait_ge(s["b_read"], B_FILLS * b + FC + 1)
                    for j in range(TILES):
                        ins = V.bn_stats(h0_st[:, j, :], h0[:, j, :])
                    step_b(ins)
                    wait(dve, "h0_scaled", 2 * b)
                    for j in range(TILES):
                        ins = V.bn_aggr(h0_mv[:, j, :], h0_st[:, j, :])
                    ins.then_inc(s["h0_stats"], 1)

                def h0_norm():
                    if B is None:
                        return
                    wait(dve, "h0_scaled", 2 * b + 2)
                    dve.wait_ge(s["h0_stats"], b + 1)
                    wait(dve, "acc_ready", b)
                    for j in range(TILES):
                        ins = V.tensor_scalar(h0n[:, j, :], h0[:, j, :], h0_mv[:, j, 0:1], h0_rstd[:, j:j + 1],
                                              ALU.subtract, ALU.mult)
                    ins.then_inc(s["h0_normed"], 1)

                def heads_divide(j):
                    if B is None:
                        return
                    wait(dve, "b_full", B_FILLS * b + OT0 + j + 1)
                    wait(dve, "b_read", B_FILLS * b + OT0 + j)
                    rows = b_ps[:].rearrange("p (h e) -> p h e", e=32)
                    step_b(V.reciprocal(row_inv[:], rows[:, :, HD]))
                    V.tensor_tensor(ao[:, j, :].rearrange("p (h e) -> p h e", e=HD), rows[:, :, 0:HD],
                                    row_inv[:].unsqueeze(2).to_broadcast([P, HEADS, HD]), ALU.mult
                                    ).then_inc(s["b_read"], 1)

                def qk_copy(fill):
                    if A is None:
                        return
                    wait(dve, "a_full", A_FILLS * a + fill + 1)
                    if fill == KT01:
                        wait(dve, k_in[1 - A[1]], 16 * LANES * (A[0] + A[1]))
                    dst = qT[A[1]] if fill == QT01 else kT
                    V.tensor_copy(dst[:, 0:2, :], a_ps[:].rearrange("p (g t) -> p g t", t=SEQ)).then_inc(s["a_read"], 1)

                def residual():
                    if B is None:
                        return
                    wait(dve, "b_full", B_FILLS * b + WO + 1)
                    wait(dve, "x1_started", b + 1)
                    V.tensor_tensor(x1[:, :, MASKED:], b_ps[:, 0:TILES * P].rearrange("p (j e) -> p j e", e=P)[:, :, 0:KEPT],
                                    x1[:, :, MASKED:], ALU.add).then_inc(s["b_read"], 1)

                def residual_scale():
                    if B is None:
                        return
                    wait(dve, "x1_scaled", 2 * b + 2)
                    wait(dve, "b_full", B_FILLS * (b - 1) + XFT + 1)
                    for j in range(TILES):
                        ins = V.tensor_scalar(xf[:, j, :], x1[:, j, :], x1_scale[:, j:j + 1], None, ALU.mult)
                    ins.then_inc(s["xf_ready"], 1)

                def ln_statistics():
                    if L is None:
                        return
                    n, p = L
                    dve.wait_ge(x_in[p], 16 * (n + 1))
                    for j in range(TILES):
                        ins = V.bn_stats(ln_st[:, j, :], x_sb[p][:, j, :])
                    step_l(ins)
                    wait(dve, "ln_scaled", l)
                    wait(dve, "xn_ready", l)
                    for j in range(TILES):
                        ins = V.bn_aggr(ln_mv[:, j, :], ln_st[:, j, :])
                    ins.then_inc(s["ln_stats"], 1)

                def ln_normalise():
                    if L is None:
                        return
                    p = L[1]
                    wait(dve, "ln_scaled", l + 1)
                    wait(dve, "x1_started", l - 1)
                    dve.wait_ge(s["ln_stats"], l + 1)
                    for j in range(TILES):
                        ins = V.tensor_scalar(xn[p][:, j, :], x_sb[p][:, j, :], ln_mv[:, j, 0:1], ln_rstd[:, j:j + 1],
                                              ALU.subtract, ALU.mult)
                    ins.then_inc(s["xn_ready"], 1)

                def down(j):
                    if C is None:
                        return
                    if j == 0:
                        wait(dve, "acc_ready", c + 1)
                    wait(dve, "down_full", TILES * c + j + 1)
                    rows = acc[C[1]][:, j, MASKED:]
                    for e in range(EXPERTS):
                        ins = V.scalar_tensor_tensor(out=rows, in0=down_ps[:, e * KEPT:(e + 1) * KEPT],
                                                     scalar=wts[:, j, e:e + 1], in1=rows, op0=ALU.mult, op1=ALU.add)
                        if e < EXPERTS - 1:
                            step_d(ins)
                    ins.then_inc(s["down_read"], 1)

                def logits_copy():
                    if B is None:
                        return
                    wait(dve, "b_full", B_FILLS * b + GATE + 1)
                    V.tensor_copy(logits[B[1]][:].rearrange("p j e -> p (j e)"), b_ps[:, 0:TILES * EXPERTS]
                                  ).then_inc(s["b_read"], 1)

                def find_maxima():
                    for r, (j, g, kt) in enumerate(ROUND_LIST):
                        wait(dve, "mx_full", ROUNDS * a + r + 1)
                        wait(dve, "mx_reduced", ROUNDS * a + r)
                        V.tensor_copy(mx_sb[:].rearrange("p l k -> p (l k)"), down_ps[:]).then_inc(s["mx_copied"], 1)
                        dve.wait_ge(s["mx_copied"], ROUNDS * a + r + 1)
                        if kt == j:
                            seen = sum(k == q for q, _, k in ROUND_LIST[:r + 1])
                            wait(dve, "mx_masked", GROUPS * TILES * a + seen)
                        V.tensor_reduce(mx[:, j, kt, LANES * g:LANES * g + LANES], mx_sb[:], AX_X, ALU.max
                                        ).then_inc(s["mx_reduced"], 1)
                    dve.wait_ge(s["mx_reduced"], ROUNDS * (a + 1))
                    V.tensor_tensor(mx[:, 1, 0, :], mx[:, 1, 0, :], mx[:, 1, 1, :], ALU.max).then_inc(s["mx_shifted"], 1)
                    dve.wait_ge(s["mx_shifted"], 2 * a + 1)
                    V.tensor_scalar(qk_parts[:, :, 0:HEADS, SHIFT], mx[:, :, 0, :], -1.0, None, ALU.mult
                                    ).then_inc(s["mx_shifted"], 1)
                    for half in range(2):
                        wait(dve, "mx_turned", 2 * a + half + 1)
                        V.tensor_copy(qT[A[1]][:, 2 * half:2 * half + 2, :], a_ps[:].rearrange("p (g t) -> p g t", t=SEQ)
                                      ).then_inc(s["mx_back"], 1)
                    V.memset(qk_parts[:, :, 0:HEADS, SHIFT:SHIFT + 1].bitcast(F32), 0.0).then_inc(s["mx_reset"], 1)
                    dve.wait_ge(s["mx_reset"], a + 1)

                gate_scores()
                a0_xsum()
                qk_square(0)
                qk_square(1)
                rsqrt_guess()
                e1_gate()
                rsqrt_newton()
                pv_copy(0)
                rsqrt_newton()
                a0_max(0)
                rsqrt_newton()
                e1_product()
                qk_norm_split()
                pv_copy(1)
                a0_max(1)
                pv_copy(2)
                a0_rows()
                pv_copy(3)
                gate_weights()
                heads_divide(0)
                h0_norm()
                heads_divide(1)
                qk_copy(QT01)
                residual()
                qk_copy(KT01)
                ln_statistics()
                residual_scale()
                down(0)
                ln_normalise()
                down(1)
                logits_copy()
                if A is not None:
                    assert count["dve_a"] == DVE_A, count
                    with dve.If(needs_max):
                        find_maxima()
                if B is not None:
                    assert count["dve_b"] == DVE_B, count

            pipeline(slot)

        @block.tensor
        def _(pe):
            T = nc.tensor

            def turn(dst, src):
                k = src.shape[0]
                return T.transpose(dst, src, ident[0:k, 0:k])

            def up(name):
                return [nat_up[name][:, m, :] for m in range(HC)]

            def square(name):
                return [nat_sq[name][:, m, ci * P:(ci + 1) * P] for ci in range(HC) for m in range(HC)]

            def dn(name):
                return [nat_dn[name][:, ci * P:(ci + 1) * P] for ci in range(HC)]

            pe.wait_ge(s["ident_ready"], 1)
            fills = [
                ("w_attn_in", 6, [nat_q[:], nat_k[:], nat_v[:]]),
                ("w_attn_in", 6, "m0"),
                ("w_attn_in", 6, [nat_fc[:], nat_wo[:]]),
                ("w_attn_in", 6, "vfc"),
                ("w_up_in", 7, up("e1a") + up("e1b")),
                ("w_up_in", 7, up("l1") + [nat_e3d[:], nat_gate[:]]),
                ("w_up_in", 7, up("e0u")),
                ("w_sq_in", 2, square("l2")),
                ("w_sq_in", 2, square("l3")),
                ("w_dn_in", 4, up("e3u") + dn("l4")),
                ("w_dn_in", 4, dn("e0d") + dn("e1d")),
                ("w_dn_in", 4, dn("e3o")),
            ]
            for f, (loaded, loads, blocks) in enumerate(fills):
                pe.wait_ge(s[loaded], 16 * loads)
                if f >= 4:
                    pe.wait_ge(s["setup_act" if f % 2 else "setup_dve"], (f - 4) // 2 + 1)
                ps = setup_ps[f % 4]
                if blocks == "m0":
                    ins = T.matmul(ps[:, 0:D], nat_qkv0[:, 0, :], nat_qkv0[:, 1, :], start=True, stop=True)
                elif blocks == "vfc":
                    pe.wait_ge(s["setup_dve"], 2)
                    ins = T.matmul(ps[:, 0:D], nat_qkv0[:, 2, :], fcT, start=True, stop=True)
                else:
                    at = 0
                    for src in blocks:
                        ins = turn(ps[:, at:at + src.shape[0]], src)
                        at += src.shape[0]
                ins.then_inc(s["setup_full"], 1)
            pe.wait_ge(s["setup_dve"], 6)
            pe.wait_ge(s["setup_act"], 6)
            pe.wait_ge(s["zeros_ready"], 4)
            pe.wait_ge(s["flag_ready"], 1)
            needs_max = pe.value_load(bounded[0:1, 0:1], min_val=0, max_val=1) == 0

            def slot(L, A, B, C):
                a, b, c = (number(t) if t is not None else None for t in (A, B, C))

                def a_fill(fill):
                    wait(pe, "a_read", A_FILLS * a + fill)

                def x_turn():
                    if A is None:
                        return
                    a_fill(XT)
                    wait(pe, "xn_ready", a + 1)
                    for j in range(TILES):
                        ins = turn(a_ps[:, j * P:(j + 1) * P], xn[A[1]][:, j, :])
                    ins.then_inc(s["a_full"], 1)

                def q0_project():
                    if A is None:
                        return
                    a_fill(Q0T)
                    T.matmul(a_ps[:, 0:SEQ], m0[:], xnT[A[1]][:], start=True, stop=True).then_inc(s["a_full"], 1)

                def qkv_project(j):
                    if A is None:
                        return
                    a_fill(QKV0 + j)
                    T.matmul(a_ps[:, 0:3 * D], xnT[A[1]][:, j * P:(j + 1) * P], qkvT[:], start=True, stop=True
                             ).then_inc(s["a_full"], 1)

                def qk_turn(fill):
                    if A is None:
                        return
                    a_fill(fill)
                    wait(pe, "qk_split", a + 1)
                    first = {QT01: 0, QT23: 8, KT01: HEADS, KT23: HEADS + 8}[fill]
                    for g in range(2):
                        for j in range(TILES):
                            heads = qk_parts[:, j, first + 4 * g:first + 4 * g + 4, :].rearrange("p h e -> p (h e)")
                            at = g * SEQ + j * P
                            ins = turn(a_ps[:, at:at + P], heads.bitcast(F32))
                    ins.then_inc(s["a_full"], 1)

                def b_fill(fill):
                    wait(pe, "b_read", B_FILLS * b + fill)

                def scores(u):
                    if B is None:
                        return
                    n, p = B
                    g, part = divmod(u, 3)
                    if u == 0:
                        wait(pe, k_in[p], 16 * LANES * (n + 1))
                        wait(pe, "a_read", A_FILLS * (b + 1))
                    wait(pe, "exp_done", UNITS * b + u - 1)
                    ps = scores_ps[u % 2]
                    if part < 2:
                        for i in range(2):
                            ins = T.matmul(ps[:, i * SEQ:(i + 1) * SEQ], k_lane[p][:, 2 * part + i, g, 0:P], qT[p][:, g, :],
                                           start=True, stop=True)
                    else:
                        for i in range(LANES):
                            ins = T.matmul(ps[:, i * P:(i + 1) * P], k_lane[p][:, i, g, P:SEQ], qT[p][:, g, P:SEQ],
                                           start=True, stop=True)
                    ins.then_inc(s["scores_full"], 1)

                def weigh_v(g):
                    if B is None:
                        return
                    n, p = B
                    wait(pe, "pv_read", GROUPS * b + g)
                    wait(pe, "probs_masked", 2 * (GROUPS * b + g) + 2)
                    wait(pe, "exp_done", UNITS * b + 3 * g + 3)
                    wait(pe, "v_ready", b + 1)
                    pr = probs[g % 2]
                    for lane in range(LANES):
                        rows = pv_ps[32 * lane:32 * lane + 32, :]
                        T.matmul(rows[:, 0:SEQ], v_aug[p][:, 0, LANES * g + lane, :], pr[:, lane, 0:SEQ], start=True,
                                 stop=False, tile_position=(0, 32 * lane))
                    for lane in range(LANES):
                        rows = pv_ps[32 * lane:32 * lane + 32, :]
                        ins = T.matmul(rows[:, P:SEQ], v_aug[p][:, 1, LANES * g + lane, :], pr[:, lane, SEQ:SEQ + P],
                                       start=False, stop=True, tile_position=(0, 32 * lane))
                    ins.then_inc(s["pv_full"], 1)

                def a0_scores(j):
                    if B is None:
                        return
                    b_fill(S00 + j)
                    p = B[1]
                    T.matmul(b_ps[:, 0:SEQ], q0T[p][:, j * P:(j + 1) * P], xnT[p][:], start=True, stop=True
                             ).then_inc(s["b_full"], 1)

                def fc_row():
                    if B is None:
                        return
                    b_fill(FC)
                    wait(pe, "xsum_ready", b + 1)
                    T.matmul(b_ps[:, 0:D], xsum_cols[:], vfc[:], start=True, stop=True).then_inc(s["b_full"], 1)

                def pv_turn(j):
                    if B is None:
                        return
                    b_fill(OT0 + j)
                    wait(pe, "pv_read", GROUPS * b + GROUPS)
                    for g in range(GROUPS):
                        ins = turn(b_ps[:, g * P:(g + 1) * P], pvT[:, g, j * P:(j + 1) * P])
                    ins.then_inc(s["b_full"], 1)

                def ao_turn():
                    if B is None:
                        return
                    b_fill(AOT)
                    for j in range(TILES):
                        ins = turn(b_ps[:, j * P:(j + 1) * P], ao[:, j, :])
                    ins.then_inc(s["b_full"], 1)

                def wo_project():
                    if B is None:
                        return
                    b_fill(WO)
                    for j in range(TILES):
                        ins = T.matmul(b_ps[:, j * P:j * P + KEPT], aoT[:, j * P:(j + 1) * P], woT[:, MASKED:], start=True,
                                       stop=True)
                    ins.then_inc(s["b_full"], 1)

                def xf_turn():
                    if B is None:
                        return
                    b_fill(XFT)
                    wait(pe, "xf_ready", b + 1)
                    for j in range(TILES):
                        ins = turn(b_ps[:, j * P:(j + 1) * P], xf[:, j, :])
                    ins.then_inc(s["b_full"], 1)

                def gate():
                    if B is None:
                        return
                    b_fill(GATE)
                    for j in range(TILES):
                        ins = T.matmul(b_ps[:, j * EXPERTS:(j + 1) * EXPERTS], xfT[B[1]][:, j * P:(j + 1) * P], gateT,
                                       start=True, stop=True)
                    ins.then_inc(s["b_full"], 1)

                def up_layer(bank, fill, wT):
                    if C is None:
                        return
                    wait(pe, f"{bank}_read", 4 * c + fill)
                    if fill == 0:
                        wait(pe, "b_read", B_FILLS * c + XFT + 1)
                    ps = even_ps if bank == "even" else odd_ps
                    for m in range(wT.shape[1] // P):
                        ins = T.matmul(ps[:, m * SEQ:(m + 1) * SEQ], wT[:, m * P:(m + 1) * P], xfT[C[1]][:], start=True,
                                       stop=True)
                    ins.then_inc(s[f"{bank}_full"], 1)

                def square_layer(fill, wT, src):
                    if C is None:
                        return
                    wait(pe, "even_read", 4 * c + fill)
                    for m in range(HC):
                        for ci in range(HC):
                            at = ci * HID + m * P
                            ins = T.matmul(even_ps[:, m * SEQ:(m + 1) * SEQ], wT[:, at:at + P], src[:, ci, :],
                                           start=(ci == 0), stop=(ci == HC - 1))
                    ins.then_inc(s["even_full"], 1)

                def e3_up_layer():
                    if C is None:
                        return
                    wait(pe, "odd_read", 4 * c + U3)
                    for m in range(HC):
                        ins = T.matmul(odd_ps[:, m * SEQ:(m + 1) * SEQ], e3u_l4T[:, m * P:(m + 1) * P], d3_h[:], start=True,
                                       stop=True)
                    ins.then_inc(s["odd_full"], 1)

                def down(j):
                    if C is None:
                        return
                    wait(pe, "down_read", TILES * c + j)
                    if j == 0:
                        wait(pe, "even_read", 4 * c + L3 + 1)
                        wait(pe, "odd_read", 4 * c + E0 + 1)
                    for e in range(EXPERTS):
                        for ci in range(HC):
                            ins = T.matmul(down_ps[:, e * KEPT:(e + 1) * KEPT], hidden[e][:, ci, j * P:(j + 1) * P],
                                           downT[e][:, ci * P + MASKED:(ci + 1) * P], start=(ci == 0), stop=(ci == HC - 1))
                    ins.then_inc(s["down_full"], 1)

                def find_maxima():
                    n, p = A
                    pe.wait_ge(k_in[p], 16 * LANES * (n + 1))
                    wait(pe, "a_read", A_FILLS * (a + 1))
                    if C is not None:
                        wait(pe, "down_read", TILES * (c + 1))
                    for r, (j, g, kt) in enumerate(ROUND_LIST):
                        wait(pe, "mx_copied", ROUNDS * a + r)
                        for lane in range(LANES):
                            ins = T.matmul(down_ps[:, lane * P:(lane + 1) * P], qT[p][:, g, j * P:(j + 1) * P],
                                           k_lane[p][:, lane, g, kt * P:(kt + 1) * P], start=True, stop=True)
                        ins.then_inc(s["mx_full"], 1)
                    wait(pe, "mx_copied", ROUNDS * (a + 1))
                    wait(pe, "mx_shifted", 2 * a + 2)
                    for half in range(2):
                        wait(pe, "mx_back", 2 * a + half)
                        for g in range(2):
                            for j in range(TILES):
                                head = 4 * (2 * half + g)
                                heads = qk_parts[:, j, head:head + 4, :].rearrange("p h e -> p (h e)")
                                at = g * SEQ + j * P
                                ins = turn(a_ps[:, at:at + P], heads.bitcast(F32))
                        ins.then_inc(s["mx_turned"], 1)
                    wait(pe, "mx_back", 2 * a + 2)
                    wait(pe, "mx_reset", a + 1)

                x_turn()
                scores(0)
                scores(1)
                qkv_project(0)
                scores(2)
                qkv_project(1)
                scores(3)
                up_layer("even", E1A, e1T[:, 0:HID])
                q0_project()
                weigh_v(0)
                scores(4)
                a0_scores(0)
                scores(5)
                up_layer("odd", E1B, e1T[:, HID:2 * HID])
                scores(6)
                weigh_v(1)
                scores(7)
                a0_scores(1)
                scores(8)
                scores(9)
                fc_row()
                weigh_v(2)
                scores(10)
                scores(11)
                weigh_v(3)
                up_layer("even", L1, l1T[:, 0:HID])
                pv_turn(0)
                up_layer("odd", D3, e3dT)
                square_layer(L2, l2T, l1_h)
                pv_turn(1)
                e3_up_layer()
                qk_turn(QT01)
                ao_turn()
                qk_turn(QT23)
                square_layer(L3, l3T, l2_h)
                wo_project()
                up_layer("odd", E0, e0uT)
                qk_turn(KT01)
                qk_turn(KT23)
                down(0)
                xf_turn()
                down(1)
                gate()
                if A is not None:
                    with pe.If(needs_max):
                        find_maxima()

            pipeline(slot)


_INS = ["L0_attn_x", "L0_attn_w_qkv", "L0_attn_w_fc", "L0_attn_b_fc", "L0_attn_gamma", "L0_attn_beta", "L0_ffn_n1_w",
        "L0_ffn_n2_w", "L0_ffn_wq", "L0_ffn_wk", "L0_ffn_wv", "L0_ffn_wo", "L0_ffn_qn_w", "L0_ffn_kn_w", "L0_ffn_gate_w",
        "L0_ffn_e0_up", "L0_ffn_e0_down", "L0_ffn_e1_w1", "L0_ffn_e1_w2", "L0_ffn_e1_down", "L0_ffn_e2_l1",
        "L0_ffn_e2_l2", "L0_ffn_e2_l3", "L0_ffn_e2_l4", "L0_ffn_e3_down", "L0_ffn_e3_up", "L0_ffn_e3_out"]


def kernel(**inputs):
    import numpy as _np
    import concourse.bacc as _bacc
    from concourse import mybir as _mybir
    from concourse.bass_utils import run_bass_kernel_spmd as _run

    nc = _bacc.Bacc("TRN2", target_bir_lowering=False, num_devices=1)
    arrays, args = {}, []
    for name in _INS:
        a = _np.ascontiguousarray(inputs[name])
        arrays[f"in_{name}"] = a
        args.append(nc.dram_tensor(f"in_{name}", a.shape, _mybir.dt.from_np(a.dtype), kind="ExternalInput").ap())
    shape = inputs["L0_attn_x"].shape
    args.append(nc.dram_tensor("out_0", shape, _mybir.dt.float32, kind="ExternalOutput").ap())
    fused_block(nc, *args)
    r = _run(nc, [arrays], core_ids=[0])
    return r.results[0]["out_0"]
```

```python
from contextlib import ExitStack

import concourse.bass as bass
from concourse import mybir

ALU = mybir.AluOpType
ACT = mybir.ActivationFunctionType
F32 = mybir.dt.float32
F32R = mybir.dt.float32r
I32 = mybir.dt.int32
BF16 = mybir.dt.bfloat16
AX_X = mybir.AxisListType.X

P = 128
FLOAT_MAX = 3.4028234663852886e38
EXP_SAFE = 60.0
MASK_OUT = -1e30
RSQRT_SEED = 0x5F3759DF

XT, QKV0, QKV1, Q0T, KT01, KT23, QT01, QT23, A_FILLS = range(9)
S00, S01, FC, OT0, OT1, AOT, WO, XFT, GATE, B_FILLS = range(10)
E1A, L1, L2, L3, EVEN_FILLS = range(5)
E1B, D3, U3, E0, ODD_FILLS = range(5)


def fused_block(nc: bass.Bass, x, w_qkv, w_fc, b_fc, gamma, beta, n1_w, n2_w, wq, wk, wv, wo, qn_w, kn_w,
                gate_w, e0_up, e0_down, e1_w1, e1_w2, e1_down, e2_l1, e2_l2, e2_l3, e2_l4, e3_down, e3_up,
                e3_out, out):
    BATCHES, SEQ, D = x.shape
    HD = qn_w.shape[0]
    HEADS = D // HD
    EXPERTS = gate_w.shape[0]
    HID = e0_up.shape[0]
    MASKED = 32
    KEPT = D - MASKED
    LN_EPS, RMS_EPS = 1e-5, 1.1920929e-07
    TILES = SEQ // P
    HC = HID // P
    LANES = 4
    GROUPS = HEADS // LANES
    UNITS = 3 * GROUPS
    SHIFT = 3 * HD
    assert D == P and TILES == 2 and HC == 2 and HD == 8 and BATCHES % 2 == 0

    with ExitStack() as ctx:
        def sb(name, shape, dt=F32):
            return ctx.enter_context(nc.sbuf_tensor(name, shape, dt))

        def psum(name):
            return ctx.enter_context(nc.psum_tensor(name, [P, 512], F32))

        def sem(name):
            return ctx.enter_context(nc.semaphore(name))

        scores_ps = [psum("scores0_ps"), psum("scores1_ps")]
        pv_ps = psum("pv_ps")
        even_ps, odd_ps = psum("even_ps"), psum("odd_ps")
        a_ps, b_ps, down_ps = psum("a_ps"), psum("b_ps"), psum("down_ps")
        setup_ps = [scores_ps[0], scores_ps[1], even_ps, odd_ps]

        nat_qkv0 = sb("nat_qkv0", [P, 3, D])
        nat_fc, nat_wo = sb("nat_fc", [P, D]), sb("nat_wo", [P, D])
        nat_q, nat_k, nat_v = sb("nat_q", [P, D]), sb("nat_k", [P, D]), sb("nat_v", [P, D])
        nat_gate = sb("nat_gate", [EXPERTS, D])
        nat_up = {n: sb(f"nat_{n}", [P, HC, D]) for n in ("e0u", "e1a", "e1b", "l1", "e3u")}
        nat_sq = {n: sb(f"nat_{n}", [P, HC, HID]) for n in ("l2", "l3")}
        nat_dn = {n: sb(f"nat_{n}", [P, HID]) for n in ("e0d", "e1d", "l4", "e3o")}
        nat_e3d = sb("nat_e3d", [P, D])

        qkvT = sb("qkvT", [P, 3 * D])
        m0 = sb("m0", [P, D])
        fcwoT = sb("fcwoT", [P, 2 * D])
        vfc = sb("vfc", [P, D])
        e1T = sb("e1T", [P, 2 * HID])
        l1T = sb("l1T", [P, HID + D + EXPERTS])
        e0uT = sb("e0uT", [P, HID])
        l2T, l3T = sb("l2T", [P, HC * HID]), sb("l3T", [P, HC * HID])
        e3u_l4T = sb("e3u_l4T", [P, 2 * HID])
        e0d_e1dT = sb("e0d_e1dT", [P, 2 * HID])
        e3oT = sb("e3oT", [P, HID])
        fcT, woT = fcwoT[:, 0:D], fcwoT[:, D:2 * D]
        e3dT, gateT = l1T[:, HID:HID + D], l1T[:, HID + D:HID + D + EXPERTS]
        downT = [e0d_e1dT[:, 0:HID], e0d_e1dT[:, HID:2 * HID], e3u_l4T[:, HID:2 * HID], e3oT[:, :]]

        ident = sb("ident", [P, P])
        n1_col, n2_col = sb("n1_col", [P, 1]), sb("n2_col", [P, 1])
        qn_row, kn_row, qk_w = sb("qn_row", [P, HD]), sb("kn_row", [P, HD]), sb("qk_w", [P, HD])
        bfc_row, gamma_row, beta_row = sb("bfc_row", [P, D]), sb("gamma_row", [P, D]), sb("beta_row", [P, D])
        minus_half = sb("minus_half", [P, TILES])
        lower = sb("lower", [P, EXPERTS, EXPERTS])
        ones = sb("ones", [P, P])
        ident_bf = sb("ident_bf", [P, P], BF16)
        mask_f = sb("mask_f", [P, P])
        later_keys = sb("later_keys", [P, P], BF16)
        later_keys_q = sb("later_keys_q", [P, P], BF16)
        widest, bounded = sb("widest", [1, 1]), sb("bounded", [1, 1], I32)
        mx = sb("mx", [P, TILES, TILES, HEADS])

        x_sb = [sb(f"x_sb{p}", [P, TILES, D]) for p in range(2)]
        ln_st = sb("ln_st", [P, TILES, 6])
        ln_mv = sb("ln_mv", [P, TILES, 2])
        ln_rstd, h_scale, ln_tmp = sb("ln_rstd", [P, TILES]), sb("h_scale", [P, TILES]), sb("ln_tmp", [P, TILES])
        xn = [sb(f"xn{r}", [P, TILES, D]) for r in range(3)]
        xnT = [sb(f"xnT{p}", [P, SEQ]) for p in range(2)]
        xn_sum = [sb(f"xn_sum{p}", [P, 1]) for p in range(2)]
        q0T = [sb(f"q0T{p}", [P, SEQ]) for p in range(2)]
        qkv = sb("qkv", [P, TILES, 3 * D])
        qk_sq = sb("qk_sq", [P, TILES, 2 * D])
        qk_ms = sb("qk_ms", [P, TILES, 2 * HEADS])
        qk_y, qk_t = sb("qk_y", [P, TILES, 2 * HEADS]), sb("qk_t", [P, TILES, 2 * HEADS])
        qk_n = sb("qk_n", [P, TILES, 2 * HEADS, HD])
        qk_parts = sb("qk_parts", [P, TILES, 2 * HEADS, 32], F32R)
        v_aug = [sb(f"v_aug{p}", [P, TILES, HEADS, 32]) for p in range(2)]
        qT = [sb(f"qT{p}", [P, GROUPS, SEQ], F32R) for p in range(2)]
        kT = sb("kT", [P, GROUPS, SEQ], F32R)
        k_lane = [sb(f"k_lane{p}", [P, LANES, GROUPS, SEQ], F32R) for p in range(2)]

        probs = [sb(f"probs{g}", [P, LANES, SEQ + P]) for g in range(2)]
        pvT = sb("pvT", [P, GROUPS, SEQ])
        row_inv = sb("row_inv", [P, TILES, HEADS])
        ao = sb("ao", [P, TILES, D])
        aoT = sb("aoT", [P, SEQ])
        a0_negmax, a0_sum = sb("a0_negmax", [P, TILES]), sb("a0_sum", [P, TILES])
        a0_inv, a0_row = sb("a0_inv", [P, TILES]), sb("a0_row", [P, TILES])
        a0_exp = sb("a0_exp", [P, SEQ])
        xsum_cols = sb("xsum_cols", [P, P])
        xn_b = sb("xn_b", [P, TILES, D])
        h0, h0n = sb("h0", [P, TILES, D]), sb("h0n", [P, TILES, D])
        h0_st, h0_mv = sb("h0_st", [P, TILES, 6]), sb("h0_mv", [P, TILES, 2])
        h0_rstd = sb("h0_rstd", [P, TILES])
        x1 = sb("x1_sb", [P, TILES, D])
        x1_ms, x1_scale = sb("x1_ms", [P, TILES]), sb("x1_scale", [P, TILES])
        x1_sq = sb("x1_sq", [P, D])
        xf = sb("xf", [P, TILES, D])
        xfT = [sb(f"xfT{p}", [P, SEQ]) for p in range(2)]
        acc = [sb(f"acc{p}", [P, TILES, D]) for p in range(2)]
        logits = [sb(f"logits{p}", [P, TILES, EXPERTS]) for p in range(2)]

        g_a, g_b, g_c = (sb(f"gate_{n}", [P, TILES, EXPERTS]) for n in "abc")
        g_m = sb("gate_m", [P, TILES])
        g_gt, g_eq = sb("gate_gt", [P, TILES, EXPERTS, EXPERTS]), sb("gate_eq", [P, TILES, EXPERTS, EXPERTS])
        wts = sb("wts", [P, TILES, EXPERTS])
        e1_t, e1_s, e1_h = (sb(f"e1_{n}", [P, HC, SEQ]) for n in "tsh")
        l1_h, l2_h, l3_h = sb("l1_h", [P, HC, SEQ]), sb("l2_h", [P, HC, SEQ]), sb("l3_h", [P, HC, SEQ])
        d3_h, u3_h, e0_h = sb("d3_h", [P, SEQ]), sb("u3_h", [P, HC, SEQ]), sb("e0_h", [P, HC, SEQ])
        hidden = [e0_h, e1_h, l3_h, u3_h]

        names = """ident_ready consts_ready n1_in qk_w_in w_heads_in w_qkv_in w_attn_in w_up_in w_sq_in w_dn_in rows_in
                   setup_full setup_dve setup_act qk_w_ready zeros_ready masks_ready flag_ready
                   mx_full mx_reduced mx_shifted mx_turned mx_back mx_reset
                   ln_stats ln_scaled xn_ready a_full a_read q_split k_split v_ready
                   scores_full exp_done pv_full pv_read
                   b_full b_read a0_maxed a0_rowed xsum_ready h0_stats h0_scaled h0_normed
                   xnb_ready x1_started x1_squared x1_scaled xf_ready acc_ready
                   gate_shifted gate_exped e1_tanh
                   even_full even_read odd_full odd_read down_full down_read
                   dve_a dve_b dve_c dve_d dve_l dve_s pool_l pool_b pool_s""".split()
        s = {n: sem(n) for n in names}
        x_in, k_in, acc_in, out_done = ([sem(f"{n}{p}") for p in range(2)] for n in ("x_in", "k_in", "acc_in", "out_done"))

        DVE_A, DVE_B, DVE_C, DVE_D, POOL_L, POOL_B = 24, 4, 15, 6, 5, 3
        ROUNDS = GROUPS * (TILES * (TILES + 1) // 2)

        ROUND_LIST = [(j, g, kt) for j in range(TILES) for g in range(GROUPS) for kt in range(j + 1)]

        block = ctx.enter_context(nc.Block())

        def wait(eng, name, value):
            if not isinstance(value, int) or value > 0:
                eng.wait_ge(s[name] if isinstance(name, str) else name, value)

        def pipeline(slot):
            slot((0, 1), (0, 0), None, None, turn_weights=True)
            slot((1, 0), (0, 1), (0, 0), None)
            for n in range(BATCHES // 2 - 2):
                slot((n + 1, 1), (n + 1, 0), (n, 1), (n, 0))
                slot((n + 2, 0), (n + 1, 1), (n + 1, 0), (n, 1))
            last = BATCHES // 2 - 1
            slot((last, 1), (last, 0), (last - 1, 1), (last - 1, 0))
            slot(None, (last, 1), (last, 0), (last - 1, 1))
            slot(None, None, (last, 1), (last, 0))
            slot(None, None, None, (last, 1))

        def number(batch):
            return 2 * batch[0] + batch[1]

        @block.sync
        def _(sp):
            sp.dma_start(x_sb[0][:], x[0].rearrange("(j p) d -> p j d", p=P)).then_inc(x_in[0], 16)
            for dst, src in ((nat_q, wq), (nat_k, wk), (nat_v, wv)):
                sp.dma_start(dst[:], src).then_inc(s["w_heads_in"], 16)
            sp.dma_start(nat_qkv0[:], w_qkv.rearrange("(c p) d -> p c d", p=P)).then_inc(s["w_qkv_in"], 16)
            sp.dma_start(x_sb[1][:], x[1].rearrange("(j p) d -> p j d", p=P)).then_inc(x_in[1], 16)
            for dst, src in ((nat_fc, w_fc), (nat_wo, wo)):
                sp.dma_start(dst[:], src).then_inc(s["w_attn_in"], 16)
            for name, src in (("e1a", e1_w1), ("e1b", e1_w2), ("l1", e2_l1), ("e0u", e0_up), ("e3u", e3_up)):
                sp.dma_start(nat_up[name][:], src.rearrange("(c p) d -> p c d", p=P)).then_inc(s["w_up_in"], 16)
            sp.dma_start(nat_e3d[:], e3_down).then_inc(s["w_up_in"], 16)
            sp.dma_start(nat_gate[:], gate_w).then_inc(s["w_up_in"], 16)
            for name, src in (("l2", e2_l2), ("l3", e2_l3)):
                sp.dma_start(nat_sq[name][:], src.rearrange("(c p) d -> p c d", p=P)).then_inc(s["w_sq_in"], 16)
            for name, src in (("e0d", e0_down), ("e1d", e1_down), ("l4", e2_l4), ("e3o", e3_out)):
                sp.dma_start(nat_dn[name][:], src).then_inc(s["w_dn_in"], 16)

            def rows_of(t, batch):
                return t[batch].rearrange("(j p) d -> p j d", p=P)

            def slot(L, A, B, C, turn_weights=False):
                if L is not None and L[0] != 0:
                    n, p = L
                    wait(sp, "xn_ready", number(L) - 1)
                    sp.dma_start(x_sb[p][:], rows_of(x, number(L))).then_inc(x_in[p], 16)
                if B is not None:
                    n, p = B
                    wait(sp, out_done[p], 16 * n)
                    sp.dma_start(acc[p][:], rows_of(x, number(B))).then_inc(acc_in[p], 16)
                if A is not None:
                    n, p = A
                    a = number(A)
                    wait(sp, "a_read", A_FILLS * a + KT23 + 1)
                    wait(sp, "scores_full", UNITS * (a - 1))
                    wait(sp, "zeros_ready", 4)
                    for lane in range(LANES):
                        rows = slice(32 * lane, 32 * lane + 32)
                        sp.dma_start(k_lane[p][rows, lane].bitcast(F32), kT[rows].bitcast(F32)).then_inc(k_in[p], 16)
                if C is not None:
                    n, p = C
                    wait(sp, "down_read", TILES * number(C) + TILES)
                    sp.dma_start(rows_of(out, number(C)), acc[p][:]).then_inc(out_done[p], 16)

            slot((0, 0), None, None, None)
            pipeline(slot)
            for p in range(2):
                sp.wait_ge(out_done[p], 16 * (BATCHES // 2))

        @block.gpsimd
        def _(pool):
            def step(ins, name, value):
                ins.then_inc(s[name], 1)
                pool.wait_ge(s[name], value)

            step(nc.gpsimd.memset(ident[:], 0.0), "pool_s", 1)
            nc.gpsimd.affine_select(out=ident[:], in_=ident[:], compare_op=ALU.not_equal, fill=1.0, base=0,
                                    pattern=[[-1, P]], channel_multiplier=1).then_inc(s["ident_ready"], 1)
            nc.gpsimd.memset(minus_half[:], -0.5)

            def constants():
                nc.gpsimd.memset(ones[:], 1.0)
                step(nc.gpsimd.memset(qk_parts[:].bitcast(F32), 0.0), "pool_s", 2)
                nc.gpsimd.memset(qk_parts[:, :, HEADS:, SHIFT:SHIFT + 1].bitcast(F32), 1.0)
                step(nc.gpsimd.memset(lower[:], 1.0), "pool_s", 3)
                nc.gpsimd.affine_select(out=lower[:], in_=lower[:], compare_op=ALU.is_gt, fill=0.0, base=0,
                                        pattern=[[1, EXPERTS], [-1, EXPERTS]], channel_multiplier=0
                                        ).then_inc(s["consts_ready"], 1)
                nc.gpsimd.memset(k_lane[0][:].bitcast(F32), 0.0).then_inc(s["zeros_ready"], 1)
                step(nc.gpsimd.memset(v_aug[0][:], 0.0), "pool_s", 4)
                nc.gpsimd.memset(v_aug[0][:, :, :, HD:HD + 1], 1.0).then_inc(s["zeros_ready"], 1)
                pool.wait_ge(s["ident_ready"], 1)
                nc.gpsimd.tensor_copy(ident_bf[:], ident[:])
                for k, (mask, sign) in enumerate(((later_keys, 1), (later_keys_q, -1))):
                    step(nc.gpsimd.memset(mask_f[:], 0.0), "pool_s", 5 + 2 * k)
                    step(nc.gpsimd.affine_select(out=mask_f[:], in_=mask_f[:], compare_op=ALU.is_ge, fill=MASK_OUT, base=0,
                                                 pattern=[[sign, P]], channel_multiplier=-sign), "pool_s", 6 + 2 * k)
                    nc.gpsimd.tensor_copy(mask[:], mask_f[:]).then_inc(s["masks_ready"], 1)
                    pool.wait_ge(s["masks_ready"], k + 1)
                step(nc.gpsimd.memset(v_aug[1][:], 0.0), "pool_s", 9)
                nc.gpsimd.memset(v_aug[1][:, :, :, HD:HD + 1], 1.0).then_inc(s["zeros_ready"], 1)
                nc.gpsimd.memset(k_lane[1][:].bitcast(F32), 0.0).then_inc(s["zeros_ready"], 1)
                pool.wait_ge(s["zeros_ready"], 3)

            def slot(L, A, B, C, turn_weights=False):
                l, a, b = (number(t) if t is not None else None for t in (L, A, B))
                k = {"pool_l": POOL_L * l if L is not None else 0, "pool_b": POOL_B * b if B is not None else 0}

                def step_of(ins, name):
                    k[name] += 1
                    ins.then_inc(s[name], 1)

                def biased():
                    if B is None:
                        return
                    wait(pool, "xn_ready", b + 1)
                    wait(pool, "b_read", B_FILLS * (b - 1) + FC + 1)
                    pool.wait_ge(s["rows_in"], 4 * 16)
                    nc.gpsimd.tensor_tensor(xn_b[:], xn[b % 3][:], bfc_row[:].unsqueeze(1).to_broadcast([P, TILES, D]),
                                            ALU.add).then_inc(s["xnb_ready"], 1)

                def x1_start():
                    if B is None:
                        return
                    wait(pool, "xn_ready", b + 1)
                    wait(pool, "acc_ready", b)
                    wait(pool, "xf_ready", b)
                    nc.gpsimd.tensor_copy(x1[:, :, 0:MASKED], xn[b % 3][:, :, 0:MASKED]).then_inc(s["x1_started"], 1)

                def v_copy():
                    if A is None:
                        return
                    wait(pool, "a_read", A_FILLS * a + QKV1 + 1)
                    wait(pool, "pv_full", GROUPS * (a - 1))
                    nc.gpsimd.tensor_copy(v_aug[A[1]][:, :, :, 0:HD],
                                          qkv[:, :, 2 * D:3 * D].rearrange("p j (h e) -> p j h e", e=HD)
                                          ).then_inc(s["v_ready"], 1)

                def h0_variance():
                    if B is None:
                        return
                    wait(pool, "h0_stats", b + 1)
                    nc.gpsimd.tensor_scalar(h0_rstd[:], h0_mv[:, :, 1], LN_EPS, 1.0, ALU.add, ALU.mult
                                            ).then_inc(s["h0_scaled"], 1)

                def h0_scale():
                    if B is None:
                        return
                    pool.wait_ge(s["h0_scaled"], 2 * b + 1)
                    nc.gpsimd.tensor_tensor(h0_rstd[:], h0_rstd[:], minus_half[:], ALU.pow
                                            ).then_inc(s["h0_scaled"], 1)

                def h0_gamma():
                    if B is None:
                        return
                    wait(pool, "h0_normed", b + 1)
                    step_of(nc.gpsimd.tensor_tensor(h0n[:], h0n[:], gamma_row[:].unsqueeze(1).to_broadcast([P, TILES, D]),
                                                    ALU.mult), "pool_b")

                def h0_beta():
                    if B is None:
                        return
                    pool.wait_ge(s["pool_b"], k["pool_b"])
                    step_of(nc.gpsimd.tensor_tensor(h0n[:], h0n[:], beta_row[:].unsqueeze(1).to_broadcast([P, TILES, D]),
                                                    ALU.add), "pool_b")

                def h0_add():
                    if B is None:
                        return
                    pool.wait_ge(acc_in[B[1]], 16 * (B[0] + 1))
                    pool.wait_ge(s["pool_b"], k["pool_b"])
                    step_of(nc.gpsimd.tensor_tensor(acc[B[1]][:], h0n[:], acc[B[1]][:], ALU.add), "pool_b")

                def x1_variance():
                    if B is None:
                        return
                    wait(pool, "x1_squared", TILES * b + TILES)
                    nc.gpsimd.tensor_scalar(x1_scale[:], x1_ms[:], RMS_EPS, 1.0, ALU.add, ALU.mult
                                            ).then_inc(s["x1_scaled"], 1)

                def x1_pow():
                    if B is None:
                        return
                    pool.wait_ge(s["x1_scaled"], 2 * b + 1)
                    nc.gpsimd.tensor_tensor(x1_scale[:], x1_scale[:], minus_half[:], ALU.pow
                                            ).then_inc(s["x1_scaled"], 1)

                def x1_add():
                    if B is None:
                        return
                    wait(pool, "b_read", B_FILLS * b + WO + 1)
                    pool.wait_ge(s["pool_b"], k["pool_b"])
                    nc.gpsimd.tensor_tensor(acc[B[1]][:], acc[B[1]][:], x1[:], ALU.add).then_inc(s["acc_ready"], 1)

                def ln_variance():
                    if L is None:
                        return
                    wait(pool, "ln_stats", l + 1)
                    wait(pool, "a_read", A_FILLS * (l - 1) + QKV1 + 1)
                    step_of(nc.gpsimd.tensor_scalar(ln_tmp[:], ln_mv[:, :, 1], LN_EPS, 1.0, ALU.add, ALU.mult), "pool_l")

                def ln_pow():
                    if L is None:
                        return
                    pool.wait_ge(s["pool_l"], k["pool_l"])
                    step_of(nc.gpsimd.tensor_tensor(ln_rstd[:], ln_tmp[:], minus_half[:], ALU.pow), "pool_l")

                def h_square():
                    if L is None:
                        return
                    pool.wait_ge(s["pool_l"], k["pool_l"])
                    step_of(nc.gpsimd.tensor_tensor(ln_tmp[:], ln_rstd[:], ln_rstd[:], ALU.mult), "pool_l")

                def h_mean():
                    if L is None:
                        return
                    pool.wait_ge(s["pool_l"], k["pool_l"])
                    step_of(nc.gpsimd.tensor_tensor(ln_tmp[:], ln_tmp[:], ln_mv[:, :, 1], ALU.mult), "pool_l")

                def h_eps():
                    if L is None:
                        return
                    pool.wait_ge(s["pool_l"], k["pool_l"])
                    step_of(nc.gpsimd.tensor_scalar(ln_tmp[:], ln_tmp[:], RMS_EPS, 1.0, ALU.add, ALU.mult), "pool_l")

                def h_pow():
                    if L is None:
                        return
                    pool.wait_ge(s["pool_l"], k["pool_l"])
                    nc.gpsimd.tensor_tensor(h_scale[:], ln_tmp[:], minus_half[:], ALU.pow
                                            ).then_inc(s["ln_scaled"], 1)

                ln_variance()
                biased()
                v_copy()
                ln_pow()
                h_square()
                h_mean()
                h_eps()
                x1_start()
                h0_variance()
                h0_scale()
                h_pow()
                h0_gamma()
                h0_beta()
                h0_add()
                x1_variance()
                x1_pow()
                x1_add()

            slot((0, 0), None, None, None)
            constants()
            pipeline(slot)

        @block.scalar
        def _(act):
            act.dma_start(n1_col[:], n1_w.rearrange("(p a) -> p a", a=1)).then_inc(s["n1_in"], 16)
            for dst, src in ((qn_row, qn_w), (kn_row, kn_w)):
                act.dma_start(dst[:], src.partition_broadcast(P)).then_inc(s["qk_w_in"], 16)
            act.dma_start(n2_col[:], n2_w.rearrange("(p a) -> p a", a=1)).then_inc(s["rows_in"], 16)
            for dst, src in ((bfc_row, b_fc), (gamma_row, gamma), (beta_row, beta)):
                act.dma_start(dst[:], src.partition_broadcast(P)).then_inc(s["rows_in"], 16)
            act.wait_ge(s["setup_full"], 2)
            nc.scalar.activation(m0[:], setup_ps[1][:, 0:D], ACT.Copy, scale=float(D) ** -0.5
                                 ).then_inc(s["setup_act"], 1)

            def slot(L, A, B, C, turn_weights=False):
                l, a, b, c = (number(t) if t is not None else None for t in (L, A, B, C))

                def exp_unit(u):
                    if B is None:
                        return
                    g, part = divmod(u, 3)
                    wait(act, "scores_full", UNITS * b + u + 1)
                    if part == 0:
                        wait(act, "pv_full", GROUPS * b + g - 1)
                    dst = (probs[g % 2][:, 0:2, 0:SEQ], probs[g % 2][:, 2:4, 0:SEQ], probs[g % 2][:, :, SEQ:SEQ + P])[part]
                    src = scores_ps[u % 2][:].rearrange("p (l q) -> p l q", q=dst.shape[2])
                    nc.scalar.activation(dst, src, ACT.Exp).then_inc(s["exp_done"], 1)

                def a0_softmax(j):
                    if B is None:
                        return
                    wait(act, "a0_maxed", TILES * b + j + 1)
                    if j == 0:
                        wait(act, "a0_rowed", b)
                    nc.scalar.activation(a0_exp[:], b_ps[:, 0:SEQ], ACT.Exp, bias=a0_negmax[:, j:j + 1],
                                         accum_out=a0_sum[:, j:j + 1]).then_inc(s["b_read"], 1)

                def x_copy():
                    if L is None:
                        return
                    p = L[1]
                    wait(act, "a_full", A_FILLS * l + XT + 1)
                    wait(act, "xsum_ready", l - 1)
                    wait(act, "b_full", B_FILLS * (l - 2) + S01 + 1)
                    nc.scalar.activation(xnT[p][:], a_ps[:, 0:SEQ], ACT.Copy, accum_out=xn_sum[p][:]
                                         ).then_inc(s["a_read"], 1)

                def q0_copy():
                    if L is None:
                        return
                    wait(act, "a_full", A_FILLS * l + Q0T + 1)
                    nc.scalar.copy(q0T[L[1]][:], a_ps[:, 0:SEQ]).then_inc(s["a_read"], 1)

                def qkv_copy(j):
                    if L is None:
                        return
                    wait(act, "a_full", A_FILLS * l + QKV0 + j + 1)
                    wait(act, "ln_scaled", l + 1)
                    wait(act, "v_ready", l)
                    wait(act, "k_split", TILES * l)
                    nc.scalar.activation(qkv[:, j, :], a_ps[:, 0:3 * D], ACT.Copy, scale=h_scale[:, j:j + 1]
                                         ).then_inc(s["a_read"], 1)

                def e1_tanh():
                    if C is None:
                        return
                    wait(act, "even_full", EVEN_FILLS * c + E1A + 1)
                    wait(act, "odd_read", ODD_FILLS * c)
                    nc.scalar.activation(e1_t[:].rearrange("p c q -> p (c q)"), even_ps[:], ACT.Tanh, scale=0.5
                                         ).then_inc(s["e1_tanh"], 1)

                def gate_exp():
                    if C is None:
                        return
                    wait(act, "gate_shifted", c + 1)
                    nc.scalar.activation(g_b[:], g_a[:], ACT.Exp).then_inc(s["gate_exped"], 1)

                def weights_copy():
                    if not turn_weights:
                        return
                    act.wait_ge(s["rows_in"], 4 * 16)
                    norm = n2_col[:, 0:1]
                    for f, (dst, scale) in enumerate(((fcwoT, 1.0), (vfc, 1.0), (e1T, norm), (l1T, norm), (e0uT, norm),
                                                      (l2T, 1.0), (l3T, 1.0), (e3u_l4T, 1.0), (e0d_e1dT, 1.0),
                                                      (e3oT, 1.0))):
                        act.wait_ge(s["setup_full"], f + 3)
                        nc.scalar.activation(dst[:], setup_ps[(f + 2) % 4][:, 0:dst.shape[1]], ACT.Copy, scale=scale
                                             ).then_inc(s["setup_act"], 1)

                def gelu(full, fill, ps, dst, done):
                    if C is None:
                        return
                    wait(act, full, 4 * c + fill + 1)
                    ncol = dst.shape[1] * (dst.shape[2] if len(dst.shape) == 3 else 1)
                    flat = dst[:].rearrange("p c q -> p (c q)") if len(dst.shape) == 3 else dst[:]
                    nc.scalar.activation(flat, ps[:, 0:ncol], ACT.Gelu).then_inc(s[done], 1)

                def q_copy():
                    if A is None:
                        return
                    wait(act, "a_full", A_FILLS * a + QT23 + 1)
                    nc.scalar.copy(qT[A[1]][:, 2:4, :], a_ps[:].rearrange("p (g t) -> p g t", t=SEQ)
                                   ).then_inc(s["a_read"], 1)

                def k_copy():
                    if A is None:
                        return
                    wait(act, "a_full", A_FILLS * a + KT23 + 1)
                    wait(act, k_in[1 - A[1]], 16 * LANES * (A[0] + A[1]))
                    nc.scalar.copy(kT[:, 2:4, :], a_ps[:].rearrange("p (g t) -> p g t", t=SEQ)).then_inc(s["a_read"], 1)

                def ao_copy():
                    if B is None:
                        return
                    wait(act, "b_full", B_FILLS * b + AOT + 1)
                    nc.scalar.copy(aoT[:], b_ps[:, 0:SEQ]).then_inc(s["b_read"], 1)

                def x1_square():
                    if B is None:
                        return
                    wait(act, "b_read", B_FILLS * b + WO + 1)
                    for j in range(TILES):
                        wait(act, "x1_squared", TILES * b + j)
                        nc.scalar.activation(x1_sq[:], x1[:, j, :], ACT.Square, scale=float(D) ** -0.5,
                                             accum_out=x1_ms[:, j:j + 1]).then_inc(s["x1_squared"], 1)

                def xf_copy():
                    if B is None:
                        return
                    wait(act, "b_full", B_FILLS * b + XFT + 1)
                    nc.scalar.copy(xfT[B[1]][:], b_ps[:, 0:SEQ]).then_inc(s["b_read"], 1)

                exp_unit(0)
                exp_unit(1)
                exp_unit(2)
                weights_copy()
                a0_softmax(0)
                exp_unit(3)
                e1_tanh()
                gate_exp()
                exp_unit(4)
                a0_softmax(1)
                exp_unit(5)
                exp_unit(6)
                exp_unit(7)
                exp_unit(8)
                exp_unit(9)
                exp_unit(10)
                exp_unit(11)
                gelu("even_full", L1, even_ps, l1_h, "even_read")
                gelu("odd_full", D3, odd_ps, d3_h, "odd_read")
                gelu("even_full", L2, even_ps, l2_h, "even_read")
                gelu("odd_full", U3, odd_ps, u3_h, "odd_read")
                ao_copy()
                k_copy()
                gelu("even_full", L3, even_ps, l3_h, "even_read")
                x1_square()
                gelu("odd_full", E0, odd_ps, e0_h, "odd_read")
                q_copy()
                x_copy()
                qkv_copy(0)
                xf_copy()
                qkv_copy(1)
                q0_copy()

            slot((0, 0), None, None, None)
            pipeline(slot)

        @block.vector
        def _(dve):
            V = nc.vector
            searching = False

            def first_weights():
                dve.wait_ge(s["n1_in"], 16)
                dve.wait_ge(s["setup_full"], 1)
                V.tensor_scalar(qkvT[:], setup_ps[0][:, 0:3 * D], n1_col[:, 0:1], None, ALU.mult).then_inc(s["setup_dve"], 1)
                dve.wait_ge(s["qk_w_in"], 2 * 16)
                V.scalar_tensor_tensor(out=qk_w[:], in0=qn_row[:], scalar=float(HD) ** -0.5, in1=kn_row[:], op0=ALU.mult,
                                       op1=ALU.mult).then_inc(s["qk_w_ready"], 1)
                dve.wait_ge(s["qk_w_ready"], 1)
                V.tensor_reduce(widest[:], qk_w[0:1, :], AX_X, ALU.max, apply_absolute_value=True).then_inc(s["dve_s"], 1)
                dve.wait_ge(s["dve_s"], 1)
                V.tensor_scalar(bounded[:], widest[:], EXP_SAFE / HD, None, ALU.is_le).then_inc(s["flag_ready"], 1)
                dve.wait_ge(s["flag_ready"], 1)
                dve.wait_ge(s["consts_ready"], 1)

            def slot(L, A, B, C, turn_weights=False):
                l, a, b, c = (number(t) if t is not None else None for t in (L, A, B, C))
                done = {"dve_a": {}, "dve_b": {}, "dve_c": {}, "dve_d": {}}
                batch_of = {"dve_a": a, "dve_b": b, "dve_c": c, "dve_d": c}
                per_batch = {"dve_a": DVE_A, "dve_b": DVE_B, "dve_c": DVE_C, "dve_d": DVE_D}

                def mark(ins, name, what):
                    done[name][what] = len(done[name]) + 1
                    ins.then_inc(s[name], 1)

                def need(name, what):
                    dve.wait_ge(s[name], batch_of[name] * per_batch[name] + done[name][what])

                def gate_finite():
                    if C is None:
                        return
                    lg = logits[C[1]]
                    wait(dve, "gate_exped", c)
                    wait(dve, "b_read", B_FILLS * (c + 1))
                    V.tensor_scalar(g_a[:], lg[:], FLOAT_MAX, -FLOAT_MAX, ALU.min, ALU.max)
                    mark(V.tensor_tensor(g_c[:], lg[:], lg[:], ALU.is_equal), "dve_c", "clamped")

                def gate_number():
                    if C is None:
                        return
                    need("dve_c", "clamped")
                    mark(V.tensor_tensor(g_a[:], g_a[:], g_c[:], ALU.mult), "dve_c", "finite")

                def gate_max():
                    if C is None:
                        return
                    need("dve_c", "finite")
                    mark(V.tensor_reduce(g_m[:], g_a[:], AX_X, ALU.max), "dve_c", "max")

                def gate_shift():
                    if C is None:
                        return
                    need("dve_c", "max")
                    V.tensor_tensor(g_a[:], g_a[:], g_m[:].unsqueeze(2).to_broadcast([P, TILES, EXPERTS]),
                                    ALU.subtract).then_inc(s["gate_shifted"], 1)

                def gate_sum():
                    if C is None:
                        return
                    wait(dve, "gate_exped", c + 1)
                    mark(V.tensor_reduce(g_m[:], g_b[:], AX_X, ALU.add), "dve_c", "sum")

                def gate_inverse():
                    if C is None:
                        return
                    need("dve_c", "sum")
                    mark(V.reciprocal(g_m[:], g_m[:]), "dve_c", "inverse")

                def gate_probs():
                    if C is None:
                        return
                    need("dve_c", "inverse")
                    mark(V.tensor_tensor(g_b[:], g_b[:], g_m[:].unsqueeze(2).to_broadcast([P, TILES, EXPERTS]),
                                         ALU.mult), "dve_c", "probs")

                def gate_compare():
                    if C is None:
                        return
                    need("dve_c", "probs")
                    for j in range(TILES):
                        other = g_b[:, j, :].unsqueeze(1).to_broadcast([P, EXPERTS, EXPERTS])
                        own = g_b[:, j, :].unsqueeze(2).to_broadcast([P, EXPERTS, EXPERTS])
                        V.tensor_tensor(g_eq[:, j], other, own, ALU.is_equal)
                        ins = V.tensor_tensor(g_gt[:, j], other, own, ALU.is_gt)
                    mark(ins, "dve_c", "compared")

                def gate_ties():
                    if C is None:
                        return
                    need("dve_c", "compared")
                    mark(V.tensor_tensor(g_eq[:], g_eq[:], lower[:].unsqueeze(1).to_broadcast(
                        [P, TILES, EXPERTS, EXPERTS]), ALU.mult), "dve_c", "tied")

                def gate_ahead():
                    if C is None:
                        return
                    need("dve_c", "tied")
                    mark(V.tensor_tensor(g_gt[:], g_gt[:], g_eq[:], ALU.add), "dve_c", "ahead")

                def gate_rank():
                    if C is None:
                        return
                    need("dve_c", "ahead")
                    mark(V.tensor_reduce(g_c[:], g_gt[:], AX_X, ALU.add), "dve_c", "rank")

                def gate_top():
                    if C is None:
                        return
                    need("dve_c", "rank")
                    mark(V.scalar_tensor_tensor(out=g_c[:], in0=g_c[:], scalar=2.0, in1=g_b[:], op0=ALU.is_lt,
                                                op1=ALU.mult), "dve_c", "top")

                def gate_top_sum():
                    if C is None:
                        return
                    need("dve_c", "top")
                    mark(V.tensor_reduce(g_m[:], g_c[:], AX_X, ALU.add), "dve_c", "top_sum")

                def gate_top_eps():
                    if C is None:
                        return
                    need("dve_c", "top_sum")
                    mark(V.tensor_scalar(g_m[:], g_m[:], 1e-8, None, ALU.add), "dve_c", "top_eps")

                def gate_top_inverse():
                    if C is None:
                        return
                    need("dve_c", "top_eps")
                    mark(V.reciprocal(g_m[:], g_m[:]), "dve_c", "top_inverse")

                def gate_weights():
                    if C is None:
                        return
                    need("dve_c", "top_inverse")
                    mark(V.tensor_tensor(wts[:], g_c[:], g_m[:].unsqueeze(2).to_broadcast([P, TILES, EXPERTS]),
                                         ALU.mult), "dve_c", "weights")

                def e1_gate():
                    if C is None:
                        return
                    wait(dve, "e1_tanh", c + 1)
                    V.scalar_tensor_tensor(out=e1_s[:].rearrange("p c q -> p (c q)"), in0=e1_t[:].rearrange("p c q -> p (c q)"),
                                           scalar=1.0, in1=even_ps[:], op0=ALU.add, op1=ALU.mult
                                           ).then_inc(s["even_read"], 1)

                def e1_product():
                    if C is None:
                        return
                    wait(dve, "even_read", EVEN_FILLS * c + E1A + 1)
                    wait(dve, "odd_full", ODD_FILLS * c + E1B + 1)
                    V.scalar_tensor_tensor(out=e1_h[:].rearrange("p c q -> p (c q)"), in0=e1_s[:].rearrange("p c q -> p (c q)"),
                                           scalar=0.5, in1=odd_ps[:], op0=ALU.mult, op1=ALU.mult
                                           ).then_inc(s["odd_read"], 1)

                def pv_copy(g):
                    if B is None:
                        return
                    wait(dve, "pv_full", GROUPS * b + g + 1)
                    if g == 0:
                        wait(dve, "b_full", B_FILLS * (b - 1) + OT1 + 1)
                    V.tensor_copy(pvT[:, g, :], pv_ps[:, 0:SEQ]).then_inc(s["pv_read"], 1)

                def qk_square(j):
                    if A is None:
                        return
                    wait(dve, "a_read", A_FILLS * a + QKV0 + j + 1)
                    mark(V.tensor_tensor(qk_sq[:, j, :], qkv[:, j, 0:2 * D], qkv[:, j, 0:2 * D], ALU.mult),
                         "dve_a", ("square", j))

                def qk_mean(j):
                    if A is None:
                        return
                    need("dve_a", ("square", j))
                    mark(V.tensor_reduce(qk_ms[:, j, :], qk_sq[:, j, :].rearrange("p (h e) -> p h e", e=HD), AX_X,
                                         ALU.add), "dve_a", ("sum", j))

                def rsqrt_input():
                    if A is None:
                        return
                    need("dve_a", ("sum", 0))
                    need("dve_a", ("sum", 1))
                    mark(V.tensor_scalar(qk_ms[:], qk_ms[:], 1.0 / HD, RMS_EPS, ALU.mult, ALU.add), "dve_a", "input")

                def rsqrt_halve():
                    if A is None:
                        return
                    need("dve_a", "input")
                    mark(V.tensor_scalar(qk_t[:].bitcast(I32), qk_ms[:].bitcast(I32), 1, None, ALU.logical_shift_right),
                         "dve_a", "halved")

                def rsqrt_guess():
                    if A is None:
                        return
                    need("dve_a", "halved")
                    mark(V.tensor_scalar(qk_y[:].bitcast(I32), qk_t[:].bitcast(I32), -1.0, float(RSQRT_SEED), ALU.mult,
                                         ALU.add), "dve_a", ("y", 0))

                def newton_square(k):
                    if A is None:
                        return
                    need("dve_a", ("y", k))
                    mark(V.tensor_tensor(qk_t[:], qk_y[:], qk_y[:], ALU.mult), "dve_a", ("yy", k))

                def newton_error(k):
                    if A is None:
                        return
                    need("dve_a", ("yy", k))
                    mark(V.scalar_tensor_tensor(out=qk_t[:], in0=qk_t[:], scalar=-0.5, in1=qk_ms[:], op0=ALU.mult,
                                                op1=ALU.mult), "dve_a", ("error", k))

                def newton_correct(k):
                    if A is None:
                        return
                    need("dve_a", ("error", k))
                    mark(V.scalar_tensor_tensor(out=qk_y[:], in0=qk_t[:], scalar=1.5, in1=qk_y[:], op0=ALU.add,
                                                op1=ALU.mult), "dve_a", ("y", k + 1))

                def qk_norm(j):
                    if A is None:
                        return
                    need("dve_a", ("y", 3))
                    mark(V.tensor_tensor(qk_n[:, j], qkv[:, j, 0:2 * D].rearrange("p (h e) -> p h e", e=HD),
                                         qk_y[:, j].unsqueeze(2).to_broadcast([P, 2 * HEADS, HD]), ALU.mult),
                         "dve_a", ("norm", j))

                def q_weight(j):
                    if A is None:
                        return
                    need("dve_a", ("norm", j))
                    mark(V.tensor_tensor(qk_n[:, j, 0:HEADS, :], qk_n[:, j, 0:HEADS, :],
                                         qk_w[:].unsqueeze(1).to_broadcast([P, HEADS, HD]), ALU.mult),
                         "dve_a", ("weight", j))

                def q_high(j):
                    if A is None:
                        return
                    wait(dve, "a_full", A_FILLS * a)
                    need("dve_a", ("weight", j))
                    highs = qk_parts[:, j, 0:HEADS, 0:2 * HD].rearrange("p h (r e) -> p h r e", e=HD)
                    mark(V.tensor_copy(highs, qk_n[:, j, 0:HEADS].unsqueeze(2).to_broadcast([P, HEADS, 2, HD])),
                         "dve_a", ("q_high", j))

                def q_low(j):
                    if A is None:
                        return
                    need("dve_a", ("q_high", j))
                    V.tensor_tensor(qk_parts[:, j, 0:HEADS, 2 * HD:3 * HD], qk_n[:, j, 0:HEADS],
                                    qk_parts[:, j, 0:HEADS, 0:HD].bitcast(F32), ALU.subtract).then_inc(s["q_split"], 1)

                def k_high(j):
                    if A is None:
                        return
                    wait(dve, "a_full", A_FILLS * a)
                    need("dve_a", ("norm", j))
                    highs = qk_parts[:, j, HEADS:, 0:4 * HD].rearrange("p h (r e) -> p h r e", e=2 * HD)[:, :, :, 0:HD]
                    mark(V.tensor_copy(highs, qk_n[:, j, HEADS:].unsqueeze(2).to_broadcast([P, HEADS, 2, HD])),
                         "dve_a", ("k_high", j))

                def k_low(j):
                    if A is None:
                        return
                    need("dve_a", ("k_high", j))
                    V.tensor_tensor(qk_parts[:, j, HEADS:, HD:2 * HD], qk_n[:, j, HEADS:],
                                    qk_parts[:, j, HEADS:, 0:HD].bitcast(F32), ALU.subtract).then_inc(s["k_split"], 1)

                def a0_max(j):
                    if B is None:
                        return
                    wait(dve, "b_full", B_FILLS * b + S00 + j + 1)
                    V.tensor_reduce(a0_negmax[:, j:j + 1], b_ps[:, 0:SEQ], AX_X, ALU.max, negate=True
                                    ).then_inc(s["a0_maxed"], 1)

                def a0_xsum():
                    if B is None:
                        return
                    wait(dve, "b_full", B_FILLS * (b - 1) + FC + 1)
                    V.tensor_scalar(xsum_cols[:], ones[:], xn_sum[B[1]][:, 0:1], None, ALU.mult).then_inc(s["xsum_ready"], 1)

                def a0_inverse():
                    if B is None:
                        return
                    wait(dve, "b_read", B_FILLS * b + S01 + 1)
                    wait(dve, "h0_normed", b)
                    mark(V.reciprocal(a0_inv[:], a0_sum[:]), "dve_b", "a0_inv")

                def a0_weight():
                    if B is None:
                        return
                    need("dve_b", "a0_inv")
                    V.tensor_tensor(a0_row[:], a0_sum[:], a0_inv[:], ALU.mult).then_inc(s["a0_rowed"], 1)

                def h0_sum():
                    if B is None:
                        return
                    wait(dve, "b_full", B_FILLS * b + FC + 1)
                    wait(dve, "xnb_ready", b + 1)
                    dve.wait_ge(s["a0_rowed"], b + 1)
                    for j in range(TILES):
                        ins = V.scalar_tensor_tensor(out=h0[:, j, :], in0=b_ps[:, 0:D], scalar=a0_row[:, j:j + 1],
                                                     in1=xn_b[:, j, :], op0=ALU.mult, op1=ALU.add)
                    ins.then_inc(s["b_read"], 1)

                def h0_statistics():
                    if B is None:
                        return
                    dve.wait_ge(s["b_read"], B_FILLS * b + FC + 1)
                    for j in range(TILES):
                        ins = V.bn_stats(h0_st[:, j, :], h0[:, j, :])
                    mark(ins, "dve_b", "h0_stats")

                def h0_moments():
                    if B is None:
                        return
                    need("dve_b", "h0_stats")
                    wait(dve, "h0_scaled", 2 * b)
                    for j in range(TILES):
                        ins = V.bn_aggr(h0_mv[:, j, :], h0_st[:, j, :])
                    ins.then_inc(s["h0_stats"], 1)

                def h0_norm():
                    if B is None:
                        return
                    wait(dve, "h0_scaled", 2 * b + 2)
                    dve.wait_ge(s["h0_stats"], b + 1)
                    wait(dve, "acc_ready", b)
                    for j in range(TILES):
                        ins = V.tensor_scalar(h0n[:, j, :], h0[:, j, :], h0_mv[:, j, 0:1], h0_rstd[:, j:j + 1],
                                              ALU.subtract, ALU.mult)
                    ins.then_inc(s["h0_normed"], 1)

                def heads_inverse(j):
                    if B is None:
                        return
                    wait(dve, "b_full", B_FILLS * b + OT0 + j + 1)
                    rows = b_ps[:].rearrange("p (h e) -> p h e", e=32)
                    mark(V.reciprocal(row_inv[:, j, :], rows[:, :, HD]), "dve_b", ("row_inv", j))

                def heads_divide(j):
                    if B is None:
                        return
                    need("dve_b", ("row_inv", j))
                    rows = b_ps[:].rearrange("p (h e) -> p h e", e=32)
                    V.tensor_tensor(ao[:, j, :].rearrange("p (h e) -> p h e", e=HD), rows[:, :, 0:HD],
                                    row_inv[:, j, :].unsqueeze(2).to_broadcast([P, HEADS, HD]), ALU.mult
                                    ).then_inc(s["b_read"], 1)

                def qk_copy(fill):
                    if A is None:
                        return
                    wait(dve, "a_full", A_FILLS * a + fill + 1)
                    if fill == KT01:
                        wait(dve, k_in[1 - A[1]], 16 * LANES * (A[0] + A[1]))
                    dst = qT[A[1]] if fill == QT01 else kT
                    V.tensor_copy(dst[:, 0:2, :], a_ps[:].rearrange("p (g t) -> p g t", t=SEQ)).then_inc(s["a_read"], 1)

                def residual():
                    if B is None:
                        return
                    wait(dve, "b_full", B_FILLS * b + WO + 1)
                    wait(dve, "x1_started", b + 1)
                    V.tensor_tensor(x1[:, :, MASKED:], b_ps[:, 0:TILES * P].rearrange("p (j e) -> p j e", e=P)[:, :, 0:KEPT],
                                    xn[b % 3][:, :, MASKED:], ALU.add).then_inc(s["b_read"], 1)

                def residual_scale():
                    if B is None:
                        return
                    wait(dve, "x1_scaled", 2 * b + 2)
                    wait(dve, "b_full", B_FILLS * (b - 1) + XFT + 1)
                    for j in range(TILES):
                        ins = V.tensor_scalar(xf[:, j, :], x1[:, j, :], x1_scale[:, j:j + 1], None, ALU.mult)
                    ins.then_inc(s["xf_ready"], 1)

                def ln_statistics():
                    if L is None:
                        return
                    n, p = L
                    dve.wait_ge(x_in[p], 16 * (n + 1))
                    for j in range(TILES):
                        ins = V.bn_stats(ln_st[:, j, :], x_sb[p][:, j, :])
                    ins.then_inc(s["dve_l"], 1)

                def ln_moments():
                    if L is None:
                        return
                    wait(dve, "dve_l", l + 1)
                    wait(dve, "ln_scaled", l)
                    wait(dve, "xn_ready", l)
                    for j in range(TILES):
                        ins = V.bn_aggr(ln_mv[:, j, :], ln_st[:, j, :])
                    ins.then_inc(s["ln_stats"], 1)

                def ln_normalise():
                    if L is None:
                        return
                    p = L[1]
                    dve.wait_ge(s["pool_l"], POOL_L * l + 2)
                    wait(dve, "x1_started", l - 2)
                    dve.wait_ge(s["ln_stats"], l + 1)
                    for j in range(TILES):
                        ins = V.tensor_scalar(xn[l % 3][:, j, :], x_sb[p][:, j, :], ln_mv[:, j, 0:1], ln_rstd[:, j:j + 1],
                                              ALU.subtract, ALU.mult)
                    ins.then_inc(s["xn_ready"], 1)

                def down(j, e):
                    if C is None:
                        return
                    if e == 0:
                        wait(dve, "acc_ready", c + 1)
                        wait(dve, "down_full", TILES * c + j + 1)
                        if j == 0:
                            need("dve_c", "weights")
                    else:
                        need("dve_d", (j, e - 1))
                    rows = acc[C[1]][:, j, MASKED:]
                    ins = V.scalar_tensor_tensor(out=rows, in0=(down_ps, pv_ps)[j][:, e * KEPT:(e + 1) * KEPT],
                                                 scalar=wts[:, j, e:e + 1], in1=rows, op0=ALU.mult, op1=ALU.add)
                    if e < EXPERTS - 1:
                        mark(ins, "dve_d", (j, e))
                    else:
                        ins.then_inc(s["down_read"], 1)

                def logits_copy():
                    if B is None:
                        return
                    wait(dve, "b_full", B_FILLS * b + GATE + 1)
                    V.tensor_copy(logits[B[1]][:].rearrange("p j e -> p (j e)"), b_ps[:, 0:TILES * EXPERTS]
                                  ).then_inc(s["b_read"], 1)

                def find_maxima():
                    for r, (j, g, kt) in enumerate(ROUND_LIST):
                        wait(dve, "mx_full", ROUNDS * a + r + 1)
                        V.tensor_reduce(mx[:, j, kt, LANES * g:LANES * g + LANES], down_ps[:].rearrange("p (l k) -> p l k", k=P),
                                        AX_X, ALU.max).then_inc(s["mx_reduced"], 1)
                    dve.wait_ge(s["mx_reduced"], ROUNDS * (a + 1))
                    V.tensor_tensor(mx[:, 1, 0, :], mx[:, 1, 0, :], mx[:, 1, 1, :], ALU.max).then_inc(s["mx_shifted"], 1)
                    dve.wait_ge(s["mx_shifted"], 2 * a + 1)
                    V.tensor_scalar(qk_parts[:, :, 0:HEADS, SHIFT], mx[:, :, 0, :], -1.0, None, ALU.mult
                                    ).then_inc(s["mx_shifted"], 1)
                    for half in range(2):
                        wait(dve, "mx_turned", 2 * a + half + 1)
                        V.tensor_copy(qT[A[1]][:, 2 * half:2 * half + 2, :], a_ps[:].rearrange("p (g t) -> p g t", t=SEQ)
                                      ).then_inc(s["mx_back"], 1)
                    V.memset(qk_parts[:, :, 0:HEADS, SHIFT:SHIFT + 1].bitcast(F32), 0.0).then_inc(s["mx_reset"], 1)
                    dve.wait_ge(s["mx_reset"], a + 1)

                a0_max(0)
                qk_square(0)
                qk_square(1)
                gate_finite()
                gate_number()
                qk_mean(0)
                qk_mean(1)
                gate_max()
                a0_xsum()
                gate_shift()
                rsqrt_input()
                rsqrt_halve()
                rsqrt_guess()
                a0_max(1)
                e1_gate()
                gate_sum()
                newton_square(0)
                gate_inverse()
                newton_error(0)
                pv_copy(0)
                gate_probs()
                newton_correct(0)
                gate_compare()
                newton_square(1)
                gate_ties()
                newton_error(1)
                gate_ahead()
                newton_correct(1)
                gate_rank()
                newton_square(2)
                newton_error(2)
                gate_top()
                newton_correct(2)
                pv_copy(1)
                qk_norm(0)
                e1_product()
                gate_top_sum()
                a0_inverse()
                k_high(0)
                qk_norm(1)
                ln_statistics()
                q_weight(0)
                q_weight(1)
                ln_moments()
                a0_weight()
                k_high(1)
                k_low(0)
                k_low(1)
                pv_copy(2)
                q_high(1)
                q_high(0)
                h0_sum()
                q_low(1)
                gate_top_eps()
                h0_statistics()
                q_low(0)
                pv_copy(3)
                ln_normalise()
                heads_inverse(0)
                gate_top_inverse()
                heads_divide(0)
                h0_moments()
                qk_copy(KT01)
                gate_weights()
                heads_inverse(1)
                heads_divide(1)
                h0_norm()
                qk_copy(QT01)
                residual()
                residual_scale()
                down(0, 0)
                down(0, 1)
                down(0, 2)
                down(0, 3)
                logits_copy()
                down(1, 0)
                down(1, 1)
                down(1, 2)
                down(1, 3)
                for name, batch in batch_of.items():
                    assert batch is None or len(done[name]) == per_batch[name], (name, done[name])
                if A is not None and searching:
                    find_maxima()

            slot((0, 0), None, None, None)
            first_weights()
            is_bounded = dve.value_load(bounded[0:1, 0:1], min_val=0, max_val=1)
            needs_max, no_max = is_bounded == 0, is_bounded == 1
            with dve.If(needs_max):
                searching = True
                pipeline(slot)
            with dve.If(no_max):
                searching = False
                pipeline(slot)

        @block.tensor
        def _(pe):
            T = nc.tensor

            def turn(dst, src):
                k = src.shape[0]
                return T.transpose(dst, src, ident[0:k, 0:k])

            def up(name):
                return [nat_up[name][:, m, :] for m in range(HC)]

            def square(name):
                return [nat_sq[name][:, m, ci * P:(ci + 1) * P] for ci in range(HC) for m in range(HC)]

            def dn(name):
                return [nat_dn[name][:, ci * P:(ci + 1) * P] for ci in range(HC)]

            pe.wait_ge(s["ident_ready"], 1)
            fills = [
                (("w_heads_in", 3), [nat_q[:], nat_k[:], nat_v[:]]),
                (("w_qkv_in", 1), "m0"),
                (("w_attn_in", 2), [nat_fc[:], nat_wo[:]]),
                (("w_attn_in", 2), "vfc"),
                (("w_up_in", 7), up("e1a") + up("e1b")),
                (("w_up_in", 7), up("l1") + [nat_e3d[:], nat_gate[:]]),
                (("w_up_in", 7), up("e0u")),
                (("w_sq_in", 2), square("l2")),
                (("w_sq_in", 2), square("l3")),
                (("w_dn_in", 4), up("e3u") + dn("l4")),
                (("w_dn_in", 4), dn("e0d") + dn("e1d")),
                (("w_dn_in", 4), dn("e3o")),
            ]

            def weights_fill(f):
                (loaded, loads), blocks = fills[f]
                pe.wait_ge(s[loaded], 16 * loads)
                if f == 4:
                    pe.wait_ge(s["setup_dve"], 1)
                elif f > 4:
                    pe.wait_ge(s["setup_act"], f - 4)
                ps = setup_ps[f % 4]
                if blocks == "m0":
                    ins = T.matmul(ps[:, 0:D], nat_qkv0[:, 0, :], nat_qkv0[:, 1, :], start=True, stop=True)
                elif blocks == "vfc":
                    pe.wait_ge(s["setup_act"], 2)
                    ins = T.matmul(ps[:, 0:D], nat_qkv0[:, 2, :], fcT, start=True, stop=True)
                else:
                    at = 0
                    for src in blocks:
                        ins = turn(ps[:, at:at + src.shape[0]], src)
                        at += src.shape[0]
                ins.then_inc(s["setup_full"], 1)

            weights_fill(0)
            weights_fill(1)
            def slot(L, A, B, C, turn_weights=False):
                l, a, b, c = (number(t) if t is not None else None for t in (L, A, B, C))

                def weights_turn():
                    if not turn_weights:
                        return
                    for f in range(2, len(fills)):
                        weights_fill(f)
                    pe.wait_ge(s["setup_act"], len(fills) - 1)
                    pe.wait_ge(s["zeros_ready"], 4)
                    pe.wait_ge(s["masks_ready"], 2)

                def a_fill(fill):
                    wait(pe, "a_read", A_FILLS * a + fill)

                def l_fill(fill):
                    wait(pe, "a_read", A_FILLS * l + fill)

                def x_turn():
                    if L is None:
                        return
                    l_fill(XT)
                    wait(pe, "xn_ready", l + 1)
                    for j in range(TILES):
                        ins = turn(a_ps[:, j * P:(j + 1) * P], xn[l % 3][:, j, :])
                    ins.then_inc(s["a_full"], 1)

                def q0_project():
                    if L is None:
                        return
                    l_fill(Q0T)
                    pe.wait_ge(s["setup_act"], 1)
                    T.matmul(a_ps[:, 0:SEQ], m0[:], xnT[L[1]][:], start=True, stop=True).then_inc(s["a_full"], 1)

                def qkv_project(j):
                    if L is None:
                        return
                    l_fill(QKV0 + j)
                    pe.wait_ge(s["setup_dve"], 1)
                    T.matmul(a_ps[:, 0:3 * D], xnT[L[1]][:, j * P:(j + 1) * P], qkvT[:], start=True, stop=True
                             ).then_inc(s["a_full"], 1)

                def qk_turn(fill):
                    if A is None:
                        return
                    a_fill(fill)
                    wait(pe, "q_split" if fill in (QT01, QT23) else "k_split", TILES * (a + 1))
                    first = {QT01: 0, QT23: 8, KT01: HEADS, KT23: HEADS + 8}[fill]
                    for g in range(2):
                        for j in range(TILES):
                            heads = qk_parts[:, j, first + 4 * g:first + 4 * g + 4, :].rearrange("p h e -> p (h e)")
                            at = g * SEQ + j * P
                            ins = turn(a_ps[:, at:at + P], heads.bitcast(F32))
                    ins.then_inc(s["a_full"], 1)

                def b_fill(fill):
                    wait(pe, "b_read", B_FILLS * b + fill)

                def scores(u):
                    if B is None:
                        return
                    n, p = B
                    g, part = divmod(u, 3)
                    if u == 0:
                        wait(pe, k_in[p], 16 * LANES * (n + 1))
                        wait(pe, "a_read", A_FILLS * (b + 1))
                    wait(pe, "exp_done", UNITS * b + u - 1)
                    ps = scores_ps[u % 2]
                    if part < 2:
                        for i in range(2):
                            T.matmul(ps[:, i * SEQ:(i + 1) * SEQ], k_lane[p][:, 2 * part + i, g, 0:P], qT[p][:, g, :],
                                     start=i == 0, stop=False)
                        own, blocks = ps[:].rearrange("p (l q) -> p l q", q=SEQ)[:, :, 0:P], 2
                    else:
                        for i in range(LANES):
                            T.matmul(ps[:, i * P:(i + 1) * P], k_lane[p][:, i, g, P:SEQ], qT[p][:, g, P:SEQ],
                                     start=i == 0, stop=False)
                        own, blocks = ps[:].rearrange("p (l q) -> p l q", q=P), LANES
                    T.matmul(own, ident_bf[:], later_keys[:].unsqueeze(1).to_broadcast([P, blocks, P]), start=False,
                             stop=True).then_inc(s["scores_full"], 1)

                def weigh_v(g):
                    if B is None:
                        return
                    n, p = B
                    wait(pe, "pv_read", GROUPS * b + g)
                    if g == 0:
                        wait(pe, "down_read", TILES * (b - 1))
                    wait(pe, "exp_done", UNITS * b + 3 * g + 3)
                    wait(pe, "v_ready", b + 1)
                    pr = probs[g % 2]
                    for lane in range(LANES):
                        rows = pv_ps[32 * lane:32 * lane + 32, :]
                        T.matmul(rows[:, 0:SEQ], v_aug[p][:, 0, LANES * g + lane, :], pr[:, lane, 0:SEQ], start=True,
                                 stop=False, tile_position=(0, 32 * lane))
                    for lane in range(LANES):
                        rows = pv_ps[32 * lane:32 * lane + 32, :]
                        ins = T.matmul(rows[:, P:SEQ], v_aug[p][:, 1, LANES * g + lane, :], pr[:, lane, SEQ:SEQ + P],
                                       start=False, stop=True, tile_position=(0, 32 * lane))
                    ins.then_inc(s["pv_full"], 1)

                def a0_scores(j):
                    if B is None:
                        return
                    b_fill(S00 + j)
                    p = B[1]
                    T.matmul(b_ps[:, 0:SEQ], q0T[p][:, j * P:(j + 1) * P], xnT[p][:], start=True, stop=True
                             ).then_inc(s["b_full"], 1)

                def fc_row():
                    if B is None:
                        return
                    b_fill(FC)
                    wait(pe, "xsum_ready", b + 1)
                    T.matmul(b_ps[:, 0:D], xsum_cols[:], vfc[:], start=True, stop=True).then_inc(s["b_full"], 1)

                def pv_turn(j):
                    if B is None:
                        return
                    b_fill(OT0 + j)
                    wait(pe, "pv_read", GROUPS * b + GROUPS)
                    for g in range(GROUPS):
                        ins = turn(b_ps[:, g * P:(g + 1) * P], pvT[:, g, j * P:(j + 1) * P])
                    ins.then_inc(s["b_full"], 1)

                def ao_turn():
                    if B is None:
                        return
                    b_fill(AOT)
                    for j in range(TILES):
                        ins = turn(b_ps[:, j * P:(j + 1) * P], ao[:, j, :])
                    ins.then_inc(s["b_full"], 1)

                def wo_project():
                    if B is None:
                        return
                    b_fill(WO)
                    for j in range(TILES):
                        ins = T.matmul(b_ps[:, j * P:j * P + KEPT], aoT[:, j * P:(j + 1) * P], woT[:, MASKED:], start=True,
                                       stop=True)
                    ins.then_inc(s["b_full"], 1)

                def xf_turn():
                    if B is None:
                        return
                    b_fill(XFT)
                    wait(pe, "xf_ready", b + 1)
                    for j in range(TILES):
                        ins = turn(b_ps[:, j * P:(j + 1) * P], xf[:, j, :])
                    ins.then_inc(s["b_full"], 1)

                def gate():
                    if B is None:
                        return
                    b_fill(GATE)
                    for j in range(TILES):
                        ins = T.matmul(b_ps[:, j * EXPERTS:(j + 1) * EXPERTS], xfT[B[1]][:, j * P:(j + 1) * P], gateT,
                                       start=True, stop=True)
                    ins.then_inc(s["b_full"], 1)

                def up_layer(bank, fill, wT):
                    if C is None:
                        return
                    wait(pe, f"{bank}_read", 4 * c + fill)
                    if fill == 0:
                        wait(pe, "b_read", B_FILLS * c + XFT + 1)
                    ps = even_ps if bank == "even" else odd_ps
                    for m in range(wT.shape[1] // P):
                        ins = T.matmul(ps[:, m * SEQ:(m + 1) * SEQ], wT[:, m * P:(m + 1) * P], xfT[C[1]][:], start=True,
                                       stop=True)
                    ins.then_inc(s[f"{bank}_full"], 1)

                def square_layer(fill, wT, src):
                    if C is None:
                        return
                    wait(pe, "even_read", 4 * c + fill)
                    for m in range(HC):
                        for ci in range(HC):
                            at = ci * HID + m * P
                            ins = T.matmul(even_ps[:, m * SEQ:(m + 1) * SEQ], wT[:, at:at + P], src[:, ci, :],
                                           start=(ci == 0), stop=(ci == HC - 1))
                    ins.then_inc(s["even_full"], 1)

                def e3_up_layer():
                    if C is None:
                        return
                    wait(pe, "odd_read", 4 * c + U3)
                    for m in range(HC):
                        ins = T.matmul(odd_ps[:, m * SEQ:(m + 1) * SEQ], e3u_l4T[:, m * P:(m + 1) * P], d3_h[:], start=True,
                                       stop=True)
                    ins.then_inc(s["odd_full"], 1)

                def down(j):
                    if C is None:
                        return
                    wait(pe, "down_read", TILES * c)
                    ps = (down_ps, pv_ps)[j]
                    if j == 1:
                        pe.wait_ge(s["pv_read"], GROUPS * min(c + 2, BATCHES))
                    if j == 0:
                        wait(pe, "even_read", 4 * c + L3 + 1)
                        wait(pe, "odd_read", 4 * c + E0 + 1)
                    for e in range(EXPERTS):
                        for ci in range(HC):
                            ins = T.matmul(ps[:, e * KEPT:(e + 1) * KEPT], hidden[e][:, ci, j * P:(j + 1) * P],
                                           downT[e][:, ci * P + MASKED:(ci + 1) * P], start=(ci == 0), stop=(ci == HC - 1))
                    ins.then_inc(s["down_full"], 1)

                def find_maxima():
                    n, p = A
                    pe.wait_ge(k_in[p], 16 * LANES * (n + 1))
                    wait(pe, "a_read", A_FILLS * (a + 1) + (Q0T + 1 if L is not None else 0))
                    if C is not None:
                        wait(pe, "down_read", TILES * (c + 1))
                    for r, (j, g, kt) in enumerate(ROUND_LIST):
                        wait(pe, "mx_reduced", ROUNDS * a + r)
                        for lane in range(LANES):
                            ins = T.matmul(down_ps[:, lane * P:(lane + 1) * P], qT[p][:, g, j * P:(j + 1) * P],
                                           k_lane[p][:, lane, g, kt * P:(kt + 1) * P], start=lane == 0, stop=kt != j and lane == LANES - 1)
                        if kt == j:
                            ins = T.matmul(down_ps[:].rearrange("p (l k) -> p l k", k=P), ident_bf[:],
                                           later_keys_q[:].unsqueeze(1).to_broadcast([P, LANES, P]), start=False, stop=True)
                        ins.then_inc(s["mx_full"], 1)
                    wait(pe, "mx_reduced", ROUNDS * (a + 1))
                    wait(pe, "mx_shifted", 2 * a + 2)
                    for half in range(2):
                        wait(pe, "mx_back", 2 * a + half)
                        for g in range(2):
                            for j in range(TILES):
                                head = 4 * (2 * half + g)
                                heads = qk_parts[:, j, head:head + 4, :].rearrange("p h e -> p (h e)")
                                at = g * SEQ + j * P
                                ins = turn(a_ps[:, at:at + P], heads.bitcast(F32))
                        ins.then_inc(s["mx_turned"], 1)
                    wait(pe, "mx_back", 2 * a + 2)
                    wait(pe, "mx_reset", a + 1)

                scores(0)
                scores(1)
                a0_scores(0)
                weights_turn()
                scores(2)
                scores(3)
                up_layer("even", E1A, e1T[:, 0:HID])
                scores(4)
                a0_scores(1)
                weigh_v(0)
                scores(5)
                scores(6)
                up_layer("odd", E1B, e1T[:, HID:2 * HID])
                weigh_v(1)
                scores(7)
                scores(8)
                scores(9)
                fc_row()
                weigh_v(2)
                scores(10)
                scores(11)
                weigh_v(3)
                up_layer("even", L1, l1T[:, 0:HID])
                up_layer("odd", D3, e3dT)
                pv_turn(0)
                qk_turn(KT01)
                square_layer(L2, l2T, l1_h)
                pv_turn(1)
                e3_up_layer()
                qk_turn(KT23)
                ao_turn()
                square_layer(L3, l3T, l2_h)
                qk_turn(QT01)
                wo_project()
                up_layer("odd", E0, e0uT)
                qk_turn(QT23)
                x_turn()
                qkv_project(0)
                down(0)
                xf_turn()
                qkv_project(1)
                down(1)
                q0_project()
                gate()
                if A is not None and searching:
                    find_maxima()

            slot((0, 0), None, None, None)
            pe.wait_ge(s["flag_ready"], 1)
            is_bounded = pe.value_load(bounded[0:1, 0:1], min_val=0, max_val=1)
            needs_max, no_max = is_bounded == 0, is_bounded == 1
            with pe.If(needs_max):
                searching = True
                pipeline(slot)
            with pe.If(no_max):
                searching = False
                pipeline(slot)

_INS = ["L0_attn_x", "L0_attn_w_qkv", "L0_attn_w_fc", "L0_attn_b_fc", "L0_attn_gamma", "L0_attn_beta", "L0_ffn_n1_w",
        "L0_ffn_n2_w", "L0_ffn_wq", "L0_ffn_wk", "L0_ffn_wv", "L0_ffn_wo", "L0_ffn_qn_w", "L0_ffn_kn_w", "L0_ffn_gate_w",
        "L0_ffn_e0_up", "L0_ffn_e0_down", "L0_ffn_e1_w1", "L0_ffn_e1_w2", "L0_ffn_e1_down", "L0_ffn_e2_l1",
        "L0_ffn_e2_l2", "L0_ffn_e2_l3", "L0_ffn_e2_l4", "L0_ffn_e3_down", "L0_ffn_e3_up", "L0_ffn_e3_out"]


def kernel(**inputs):
    import numpy as _np
    import concourse.bacc as _bacc
    from concourse import mybir as _mybir
    from concourse.bass_utils import run_bass_kernel_spmd as _run

    nc = _bacc.Bacc("TRN2", target_bir_lowering=False, num_devices=1)
    arrays, args = {}, []
    for name in _INS:
        a = _np.ascontiguousarray(inputs[name])
        arrays[f"in_{name}"] = a
        args.append(nc.dram_tensor(f"in_{name}", a.shape, _mybir.dt.from_np(a.dtype), kind="ExternalInput").ap())
    shape = inputs["L0_attn_x"].shape
    args.append(nc.dram_tensor("out_0", shape, _mybir.dt.float32, kind="ExternalOutput").ap())
    fused_block(nc, *args)
    r = _run(nc, [arrays], core_ids=[0])
    return r.results[0]["out_0"]
```
